# Optimizing a Trainium2 kernel written in Bass

```python
import numpy as np
import jax
import jax.numpy as jnp

def _softmax(x, axis=-1):
    return jax.nn.softmax(x, axis=axis)

def _gelu(x):
    return jax.nn.gelu(x, approximate=True)

def _silu(x):
    return jax.nn.silu(x)

def _sigmoid(x):
    return jax.nn.sigmoid(x)

def _layernorm(x, axis=-1, eps=1e-05):
    m = jnp.mean(x, axis=axis, keepdims=True)
    v = jnp.var(x, axis=axis, keepdims=True)
    return (x - m) / jnp.sqrt(v + eps)

def _scatter_add(tgt, idx, src, axis=0):
    return tgt.at[idx].add(src)

def _segment_sum(src, seg, n):
    return jax.ops.segment_sum(src, seg, n)
kernel_name = 'mk_xattn_ffn_d1_seqx_r8_5aa94e'

def setup_inputs(seed: int=0):
    np.random.seed(seed)
    _w = jnp.asarray

    def _rec_inputs():
        import jax
        import jax.numpy as jnp
        _rk = jax.random.key(seed)
        x = -0.0003929 + 0.9999 * jax.random.normal(jax.random.fold_in(_rk, 1), (64, 64, 256), jnp.float32)
        _lenS = 64 - jax.random.randint(jax.random.fold_in(_rk, 7), (64,), 0, max(1, 64 // 4) + 1, jnp.int32)
        _lenS2 = 64 - jax.random.randint(jax.random.fold_in(_rk, 8), (64,), 0, max(1, 64 // 4) + 1, jnp.int32)
        _ctx_1024P = jax.random.normal(jax.random.fold_in(_rk, 11), (64, 16, 128), jnp.float32)
        _ctx_1024c = jax.random.dirichlet(jax.random.fold_in(_rk, 511), 0.3 * jnp.ones((16,), jnp.float32), (64, 64))
        _ctx_1024t = jnp.einsum('bsk,bkd->bsd', _ctx_1024c, _ctx_1024P)
        _ctx_1024t = _ctx_1024t * jax.lax.rsqrt(jnp.mean(jnp.square(_ctx_1024t)) + 1e-12) * 0.953939
        ctx_1024 = -0.000494167 + 1.00018 * (_ctx_1024t + 0.3 * jax.random.normal(jax.random.fold_in(_rk, 611), (64, 64, 128), jnp.float32))
        _validS = jnp.arange(64)[None, :] < _lenS[:, None]
        _validS2 = jnp.arange(64)[None, :] < _lenS2[:, None]
        _causal = jnp.tril(jnp.ones((64, 64), dtype=bool))
        mask_BxS2_bf1 = jnp.ones((64, 64), dtype=bool)
        return (x, ctx_1024, mask_BxS2_bf1)
    x, ctx_1024, mask_BxS2_bf1 = _rec_inputs()

    def _L0_xattn_setup():
        import jax, jax.numpy as jnp
        import numpy as np
        N_HEADS = 16
        N_KV_HEADS = 8
        HEAD_DIM = 128
        D_TEXT = 256
        D_VISION = 128
        GROUPS = N_HEADS // N_KV_HEADS
        key = jax.random.key(seed)
        ks = jax.random.split(key, 6)
        B, T_text, T_vis = (4, 256, 72)
        text_hidden = jax.random.normal(ks[0], (B, T_text, D_TEXT), dtype=jnp.float32)
        vision_tokens = jax.random.normal(ks[1], (B, T_vis, D_VISION), dtype=jnp.float32)
        vision_mask = jnp.ones((B, T_vis), dtype=bool)
        s = 0.02
        Wq = jax.random.normal(ks[2], (D_TEXT, N_HEADS * HEAD_DIM), dtype=jnp.float32) * s
        Wk = jax.random.normal(ks[3], (D_VISION, N_KV_HEADS * HEAD_DIM), dtype=jnp.float32) * s
        Wv = jax.random.normal(ks[4], (D_VISION, N_KV_HEADS * HEAD_DIM), dtype=jnp.float32) * s
        Wo = jax.random.normal(ks[5], (N_HEADS * HEAD_DIM, D_TEXT), dtype=jnp.float32) * s
        return {'text_hidden': text_hidden, 'vision_tokens': vision_tokens, 'vision_mask': vision_mask, 'Wq': Wq, 'Wk': Wk, 'Wv': Wv, 'Wo': Wo}
    _L0_xattn_all = _L0_xattn_setup()
    _L0_xattn_in = {k: v for k, v in _L0_xattn_all.items() if k in ('Wq', 'Wk', 'Wv', 'Wo')}
    del _L0_xattn_all

    def _L0_ffn_setup():
        import jax, jax.numpy as jnp
        import numpy as np
        D = 256
        H = 16
        KV = 4
        DH = 128
        RD = 64
        E = 8
        TOPK = 2
        I = 128
        EPS = 1e-06
        THETA = 1000000.0

        def rmsnorm(h, w, eps=EPS):
            dt = h.dtype
            h32 = h.astype(jnp.float32)
            var = jnp.mean(h32 * h32, axis=-1, keepdims=True)
            return (w * (h32 * jax.lax.rsqrt(var + eps))).astype(dt)

        def rotate_half(t):
            half = t.shape[-1] // 2
            return jnp.concatenate([-t[..., half:], t[..., :half]], axis=-1)
        key = jax.random.key(seed)
        ks = jax.random.split(key, 16)
        s = lambda k, shape, sc: jax.random.normal(k, shape, dtype=jnp.float32) * sc
        B, S = (1, 256)
        return {'x': s(ks[0], (B, S, D), 1.0), 'ln1_w': jnp.ones((D,), jnp.float32), 'ln2_w': jnp.ones((D,), jnp.float32), 'wq': s(ks[1], (D, H * DH), 0.02), 'wk': s(ks[2], (D, KV * DH), 0.02), 'wv': s(ks[3], (D, KV * DH), 0.02), 'wo': s(ks[4], (H * DH, D), 0.02), 'qnorm_w': jnp.ones((H * DH,), jnp.float32), 'knorm_w': jnp.ones((KV * DH,), jnp.float32), 'router_w': s(ks[5], (D, E), 0.02), 'router_bias': s(ks[6], (E,), 0.1), 'wg': s(ks[7], (E, D, I), 0.02), 'wu': s(ks[8], (E, D, I), 0.02), 'wd': s(ks[9], (E, I, D), 0.02)}
    _L0_ffn_all = _L0_ffn_setup()
    _L0_ffn_in = {k: v for k, v in _L0_ffn_all.items() if k in ('ln1_w', 'ln2_w', 'wq', 'wk', 'wv', 'wo', 'qnorm_w', 'knorm_w', 'router_w', 'router_bias', 'wg', 'wu', 'wd')}
    del _L0_ffn_all
    return {'x': x, 'ctx_1024': ctx_1024, 'mask_BxS2_bf1': mask_BxS2_bf1, 'L0_xattn_Wq': _L0_xattn_in['Wq'], 'L0_xattn_Wk': _L0_xattn_in['Wk'], 'L0_xattn_Wv': _L0_xattn_in['Wv'], 'L0_xattn_Wo': _L0_xattn_in['Wo'], 'L0_ffn_ln1_w': _L0_ffn_in['ln1_w'], 'L0_ffn_ln2_w': _L0_ffn_in['ln2_w'], 'L0_ffn_wq': _L0_ffn_in['wq'], 'L0_ffn_wk': _L0_ffn_in['wk'], 'L0_ffn_wv': _L0_ffn_in['wv'], 'L0_ffn_wo': _L0_ffn_in['wo'], 'L0_ffn_qnorm_w': _L0_ffn_in['qnorm_w'], 'L0_ffn_knorm_w': _L0_ffn_in['knorm_w'], 'L0_ffn_router_w': _L0_ffn_in['router_w'], 'L0_ffn_router_bias': _L0_ffn_in['router_bias'], 'L0_ffn_wg': _L0_ffn_in['wg'], 'L0_ffn_wu': _L0_ffn_in['wu'], 'L0_ffn_wd': _L0_ffn_in['wd']}

def reference(x, ctx_1024, mask_BxS2_bf1, L0_xattn_Wq, L0_xattn_Wk, L0_xattn_Wv, L0_xattn_Wo, L0_ffn_ln1_w, L0_ffn_ln2_w, L0_ffn_wq, L0_ffn_wk, L0_ffn_wv, L0_ffn_wo, L0_ffn_qnorm_w, L0_ffn_knorm_w, L0_ffn_router_w, L0_ffn_router_bias, L0_ffn_wg, L0_ffn_wu, L0_ffn_wd):
    import jax
    import jax.numpy as jnp

    def _L0_xattn_ref(text_hidden, vision_tokens, vision_mask, Wq, Wk, Wv, Wo):
        import jax, jax.numpy as jnp
        import numpy as np
        N_HEADS = 16
        N_KV_HEADS = 8
        HEAD_DIM = 128
        D_TEXT = 256
        D_VISION = 128
        GROUPS = N_HEADS // N_KV_HEADS
        B, T_text, _ = text_hidden.shape
        T_vis = vision_tokens.shape[1]
        scale = jnp.float32(np.sqrt(HEAD_DIM))
        q = (text_hidden @ Wq).reshape(B, T_text, N_HEADS, HEAD_DIM).transpose(0, 2, 1, 3)
        k = (vision_tokens @ Wk).reshape(B, T_vis, N_KV_HEADS, HEAD_DIM).transpose(0, 2, 1, 3)
        v = (vision_tokens @ Wv).reshape(B, T_vis, N_KV_HEADS, HEAD_DIM).transpose(0, 2, 1, 3)
        k = jnp.repeat(k, GROUPS, axis=1)
        v = jnp.repeat(v, GROUPS, axis=1)
        scores = jnp.einsum('bhtd,bhsd->bhts', q, k) / scale
        mask = vision_mask[:, None, None, :]
        scores = jnp.where(mask, scores, -jnp.inf)
        attn = jax.nn.softmax(scores, axis=-1)
        attn = jnp.nan_to_num(attn, nan=0.0)
        out = jnp.einsum('bhts,bhsd->bhtd', attn, v)
        out = out.transpose(0, 2, 1, 3).reshape(B, T_text, N_HEADS * HEAD_DIM)
        return out @ Wo

    def _L0_ffn_ref(x, ln1_w, ln2_w, wq, wk, wv, wo, qnorm_w, knorm_w, router_w, router_bias, wg, wu, wd):
        import jax, jax.numpy as jnp
        import numpy as np
        D = 256
        H = 16
        KV = 4
        DH = 128
        RD = 64
        E = 8
        TOPK = 2
        I = 128
        EPS = 1e-06
        THETA = 1000000.0

        def rmsnorm(h, w, eps=EPS):
            dt = h.dtype
            h32 = h.astype(jnp.float32)
            var = jnp.mean(h32 * h32, axis=-1, keepdims=True)
            return (w * (h32 * jax.lax.rsqrt(var + eps))).astype(dt)

        def rotate_half(t):
            half = t.shape[-1] // 2
            return jnp.concatenate([-t[..., half:], t[..., :half]], axis=-1)
        B, S, _ = x.shape
        res = x
        h = rmsnorm(x, ln1_w)
        q = h @ wq
        k = h @ wk
        v = h @ wv
        q = rmsnorm(q, qnorm_w)
        k = rmsnorm(k, knorm_w)
        q = q.reshape(B, S, H, DH).transpose(0, 2, 1, 3)
        k = k.reshape(B, S, KV, DH).transpose(0, 2, 1, 3)
        v = v.reshape(B, S, KV, DH).transpose(0, 2, 1, 3)
        pos = jnp.arange(S, dtype=jnp.float32)
        inv_freq = 1.0 / THETA ** (jnp.arange(0, RD, 2, dtype=jnp.float32) / RD)
        ang = pos[:, None] * inv_freq[None, :]
        emb = jnp.concatenate([ang, ang], axis=-1)
        cos, sin = (jnp.cos(emb), jnp.sin(emb))

        def rope(t):
            rot, pas = (t[..., :RD], t[..., RD:])
            rot = rot * cos + rotate_half(rot) * sin
            return jnp.concatenate([rot, pas], axis=-1)
        q, k = (rope(q), rope(k))
        rep = H // KV
        k = jnp.repeat(k, rep, axis=1)
        v = jnp.repeat(v, rep, axis=1)
        scores = jnp.einsum('bhqd,bhkd->bhqk', q, k) / np.sqrt(DH)
        causal = jnp.tril(jnp.ones((S, S), dtype=bool))
        scores = jnp.where(causal, scores, jnp.finfo(jnp.float32).min)
        attn = jax.nn.softmax(scores.astype(jnp.float32), axis=-1).astype(q.dtype)
        o = jnp.einsum('bhqk,bhkd->bhqd', attn, v)
        o = o.transpose(0, 2, 1, 3).reshape(B, S, H * DH) @ wo
        x1 = res + o
        h2 = rmsnorm(x1, ln2_w)
        t = h2.reshape(-1, D)
        T = t.shape[0]
        logits = t.astype(jnp.float32) @ router_w
        sig = jax.nn.sigmoid(logits)
        _, topi = jax.lax.top_k(sig + router_bias, TOPK)
        aff = jnp.take_along_axis(sig, topi, axis=-1)
        aff = aff / jnp.sum(aff, axis=-1, keepdims=True)
        combine = jnp.zeros((T, E), jnp.float32).at[jnp.arange(T)[:, None], topi].set(aff)
        gate = jnp.einsum('td,edi->tei', t, wg)
        up = jnp.einsum('td,edi->tei', t, wu)
        act = jax.nn.silu(gate) * up
        moe = jnp.einsum('te,tei,eid->td', combine.astype(t.dtype), act, wd)
        return x1 + moe.reshape(B, S, D)
    x = x + _L0_xattn_ref(_layernorm(x, axis=-1), ctx_1024, mask_BxS2_bf1, L0_xattn_Wq, L0_xattn_Wk, L0_xattn_Wv, L0_xattn_Wo)
    x = x + _L0_ffn_ref(_layernorm(x, axis=-1), L0_ffn_ln1_w, L0_ffn_ln2_w, L0_ffn_wq, L0_ffn_wk, L0_ffn_wv, L0_ffn_wo, L0_ffn_qnorm_w, L0_ffn_knorm_w, L0_ffn_router_w, L0_ffn_router_bias, L0_ffn_wg, L0_ffn_wu, L0_ffn_wd)
    return x

_drawn_inputs = setup_inputs


def setup_inputs(seed=0):
    import zlib

    import numpy as np

    out = dict(_drawn_inputs(seed))
    spreads = {'L0_ffn_ln1_w': (1.0, 0.6),
     'L0_ffn_ln2_w': (1.0, 0.6),
     'L0_ffn_qnorm_w': (1.0, 0.6),
     'L0_ffn_knorm_w': (1.0, 0.6)}
    factors = {'L0_xattn_Wq': 8.0,
     'L0_xattn_Wk': 8.0,
     'L0_ffn_router_w': 8.0,
     'L0_ffn_router_bias': 8.0,
     'L0_ffn_wg': 8.0,
     'L0_ffn_wu': 8.0,
     'L0_ffn_wd': 8.0}
    for name, (base, spread) in spreads.items():
        noise = np.random.default_rng([zlib.crc32(name.encode()), seed]).standard_normal(out[name].shape)
        drawn = base * np.exp(spread * noise) if base else spread * noise
        out[name] = jnp.asarray(drawn.astype(out[name].dtype))
    for name, factor in factors.items():
        out[name] = (out[name] * factor).astype(out[name].dtype)
    return out
```

```python
from contextlib import ExitStack

import concourse.bass as bass
from concourse import mybir

ALU = mybir.AluOpType
ACT = mybir.ActivationFunctionType
F32 = mybir.dt.float32
F32R = mybir.dt.float32r
BF16 = mybir.dt.bfloat16
I32 = mybir.dt.int32
U8 = mybir.dt.uint8
AX_X = mybir.AxisListType.X

P = 128
B, S, D = 64, 64, 256
DV = 128
H, HD = 16, 128
KVX, KVS = 8, 4
E, FI = 8, 128
TOPK = 2
RD = 64
HALF = RD // 2
KD = D // P
TILES = B * S // P
GT = 2
GROUPS = TILES // GT
GTOK = GT * P
STEPS = 4
PASSES = TILES // STEPS
NPAIR = H // 2
KPAIR = KVS // 2
K_BLOCKS = 2 + 2 * 4 * 2 * 2
SCORE_SCALE = 1.0 / float(HD) ** 0.5
MASKED = -1e30
LN_EPS = 1e-5
RMS_EPS = 1e-6
RSQRT_SEED = float(0x5F3759DF)
NEWTON = 3
RSQRT_LINKS = 2 + 3 * NEWTON

N_NORM_W = 2 * KD + H + KVS

CT = 4
CHUNKS = TILES // CT
CTOK = CT * P

CROSS, SELF = 0, 1
NORM_LINKS = {CROSS: 3 + RSQRT_LINKS, SELF: 5 + RSQRT_LINKS}
TAIL_LINKS = {CROSS: 5 + RSQRT_LINKS, SELF: 2}
SUM_LINKS = {CROSS: 3, SELF: 2}
PROJ = {CROSS: NPAIR, SELF: KPAIR + NPAIR + GT}
ROTS = KPAIR + NPAIR
ADDS = ROTS - 2
RK_LINKS = RSQRT_LINKS + 1
RQ_LINKS = RSQRT_LINKS + 1
ROUTE_LINKS = 12


def need(eng, sem, value):
    if type(value) is int and value <= 0:
        return
    eng.wait_ge(sem, value)


def is_there(index, count):
    return type(index) is not int or index < count


class Chain:

    def __init__(self, eng, sem, run, links):
        self.eng, self.sem, self.run, self.links, self.k = eng, sem, run, links, 0

    def link(self, ins):
        self.k += 1
        ins.then_inc(self.sem, 1)
        self.eng.wait_ge(self.sem, self.run * self.links + self.k)

    def last(self, ins):
        self.k += 1
        ins.then_inc(self.sem, 1)
        assert self.k == self.links, (self.k, self.links)


def adds_before(j):
    return 1 if j < KPAIR else KPAIR - 1 + max(j - KPAIR, 1)


def flat(ap):
    return ap.rearrange("p h c -> p (h c)")


def build(nc, x, ctx_in, mask, Wq, Wk, Wv, Wo, ln1_w, ln2_w, wq, wk, wv, wo, qnorm_w, knorm_w,
          router_w, router_bias, wg, wu, wd, eye, rope, causal, earlier, out):
    x1_dram = nc.dram_tensor("x1_scratch", [B * S, D], F32, kind="Internal").ap()
    y_dram = nc.dram_tensor("y_scratch", [B * S, D], F32, kind="Internal").ap()
    y1_dram = nc.dram_tensor("y1_scratch", [B * S, D], F32, kind="Internal").ap()

    with ExitStack() as stack:
        def sb(name, shape, dt=F32):
            return stack.enter_context(nc.sbuf_tensor(name, shape, dt))

        def psum(name):
            return stack.enter_context(nc.psum_tensor(name, [P, 512], F32))

        def sem(name):
            return stack.enter_context(nc.semaphore(name))

        def sems(tag, names):
            return {name: sem(f"{name}_{tag}") for name in names}

        W = sb("weights", [P, 20480], F32R)
        hT = sb("hT", [P, 2, KD, GTOK], F32R)
        PT = sb("PT", [P, 2, NPAIR * P], F32R)
        U = sb("U", [P, 2, 2, NPAIR, P], F32R)
        V = sb("V", [P, STEPS, 2, KVS * HD], F32R)
        W_q = W[:, 0:8192].rearrange("p (l k c) -> p l k c", l=2, k=KD)
        W_o = W[:, 8192:16384].rearrange("p (h l c) -> p h l c", h=H, l=2)
        W_k = W[:, 16384:18432].rearrange("p (l k c) -> p l k c", l=2, k=KD)
        W_v = W[:, 18432:20480].rearrange("p (l k c) -> p l k c", l=2, k=KD)
        W_g = W[:, 0:4096].rearrange("p (l k c) -> p l k c", l=2, k=KD)
        W_u = W[:, 4096:8192].rearrange("p (l k c) -> p l k c", l=2, k=KD)
        W_d = W[:, 8192:12288].rearrange("p (l e c) -> p l e c", l=2, e=E)
        h2T = W[:, 12288:16384].rearrange("p (u l k c) -> p u l k c", u=2, l=2, k=KD)
        actT = W[:, 16384:18432].rearrange("p (u l c) -> p u l c", u=2, l=2)

        qT = sb("qT", [P, 2, 2 * GT, H, S])
        k_blocks = sb("k_blocks", [P, K_BLOCKS, S])
        kT = k_blocks[:, 1:K_BLOCKS - 1].rearrange("p (u h b) c -> p u h (b c)", u=2, h=4)
        prob = sb("prob", [P, 2, NPAIR, 2, S])
        xin = sb("xin", [P, 2, GT, D])
        xn = sb("xn", [P, GT, D])
        res = sb("res", [P, 2, GT, D])
        half_sum = sb("half_sum", [P, D])
        summed = sb("summed", [P, 2, D])
        ln_out = sb("ln_out", [P, 2, D])
        sq = sb("sq", [P, 2, 512])
        mask_rot = sb("mask_rot", [P, 2, 512])
        mask_all = mask_rot[:].rearrange("p a c -> p (a c)").bitcast(U8)
        rot = mask_rot[0:RD]
        acc_q = sb("acc_q", [P, 2, GTOK])
        acc_k = sb("acc_k", [P, 2, GTOK])
        ctx_raw = acc_q[:].rearrange("p u (t c) -> p u t c", t=GT)
        diag = sb("diag", [P, GT, P])
        any_valid = sb("any_valid", [P, B])
        mask_row = sb("mask_row", [1, 2, P], BF16)
        eye_f = sb("eye_f", [P, P])
        ones_f = sb("ones_f", [P, P])
        ones_row = sb("ones_row", [1, P], BF16)
        causal_f = sb("causal_f", [S, S])
        causal_b = sb("causal_b", [S, S], BF16)
        eye2_b = sb("eye2_b", [S, 2, S], BF16)
        cos_t = sb("cos_t", [RD, GTOK])
        sin_t = sb("sin_t", [RD, GTOK])
        norm_rows_w = sb("norm_rows_w", [N_NORM_W, P])
        norm_w = sb("norm_w", [P, N_NORM_W])
        ln_w = norm_w[:, 0:2 * KD].rearrange("p (n k) -> p n k", n=2)
        qk_w = norm_w[:, 2 * KD:]
        rt_raw = sb("rt_raw", [P, KD, E])
        rt_w = sb("rt_w", [P, KD, E])
        rt_bias = sb("rt_bias", [P, E])
        before = sb("before", [P, E, E])
        stat6 = sb("stat6", [P, CT, 6])
        stat = sb("stat", [P, CT, 2])
        tstat6 = sb("tstat6", [P, 6])
        tstat = sb("tstat", [P, 2])
        mx = sb("mx", [P, 2, 2, NPAIR])
        sm = sb("sm", [P, 2, 2, NPAIR])
        rs_v, rs_t, rs_y = sb("rs_v", [P, CT]), sb("rs_t", [P, CT]), sb("rs_y", [P, CT], I32)
        ts_v, ts_t, ts_y = sb("ts_v", [P, CT]), sb("ts_t", [P, CT]), sb("ts_y", [P, CT], I32)
        q_factor = sb("q_factor", [P, 2, 2 * GT])
        route = sb("route", [P, 5, CT, E])
        rank3 = acc_k[:].rearrange("p u (t c) -> p u t c", t=CT)
        comb = sb("comb", [P, 2, CT, E])

        q_flat = [qT[:, i].rearrange("p b h c -> p (b h c)") for i in range(2)]
        Wo_raw = q_flat[1].rearrange("p (h c) -> p h c", h=H)
        fold_T = prob[:].rearrange("p u j b c -> p u (j b c)")
        yc = kT
        xc = fold_T.rearrange("p u (t d) -> p u t d", d=D)
        total = q_flat[0][:, 0:2048].rearrange("p (u t d) -> p u t d", u=2, t=CT)
        h_full = q_flat[0][:, 2048:4096].rearrange("p (u k c) -> p u k c", u=2, k=KD)
        th = q_flat[1][:, 0:1024].rearrange("p (u c) -> p u c", u=2)
        gated = q_flat[1][:, 1024:2048].rearrange("p (u c) -> p u c", u=2)
        act_f = q_flat[1][:, 2048:3072].rearrange("p (u c) -> p u c", u=2)
        yn = q_flat[1][:, 3072:4096].rearrange("p (t d) -> p t d", t=CT)

        b_score = [psum(f"b_score{i}") for i in range(2)]
        b_pv = [psum(f"b_pv{i}") for i in range(2)]
        b_proj = [psum(f"b_proj{i}") for i in range(2)]
        b_out = psum("b_out")
        b_misc = psum("b_misc")

        NAMES = ["x_in0", "x_in1", "c_in0", "c_in1", "r_in0", "r_in1", "sum_st0", "sum_st1", "ln_st0",
                 "ln_st1", "norm_rows", "hT_ps", "hT_hi", "hT_lo", "cT_ps", "cT", "c_hi", "c_lo",
                 "proj_ps", "proj_ev", "v_lo", "cross", "rot_cos", "rotated", "sq_added", "score_ps",
                 "row_max", "shifted", "expd", "row_sum", "probs", "mask_st", "pT_ps", "pT_hi", "pT_lo",
                 "pv_ps", "u_hi", "u_lo", "out_ps", "tail", "ssk_ps", "rk_done", "rkb_ps", "k_scaled",
                 "ssq_ps", "rq_done"]
        att = [sems("x", NAMES), sems("s", NAMES)]
        eye_in, consts_in = sem("eye_in"), sem("consts_in")
        w_in = sems("in", ["Wk", "Wv", "Wq", "Wo", "wk", "wv", "wq", "wo", "wg", "wu", "wd"])
        pr = sems("prep", ["consts", "wkvT_ps", "wkvT", "wqT_ps", "wqT", "fold_ps", "fold_hi", "fold_lo",
                           "hi_s", "lo_s", "lo_wo", "hi_e", "lo_e", "lo_wd", "rt_w", "normT_ps", "normT"])
        ex = sems("e", ["y_in0", "y_in1", "x_in0", "x_in1", "st0", "st1", "norm_rows", "T_ps", "h_full",
                        "h_hi", "h_lo", "rt_ps", "rt_exp", "routed", "gate_ps", "up_ps", "tanh", "gated",
                        "act", "a_hi", "a_lo", "down_ps", "added", "init"])
        N_CONSTS = 11 * 16

        def rsqrt(ch, var, v, t, y, n, eps, scale=1.0):
            v, t, y = v[:, 0:n], t[:, 0:n], y[:, 0:n]
            yf = y.bitcast(F32)
            ch.link(nc.vector.tensor_scalar(v, var, scale, eps, ALU.mult, ALU.add))
            ch.link(nc.vector.tensor_scalar(y, v.bitcast(I32), -0.5, RSQRT_SEED, ALU.mult, ALU.add))
            for _ in range(NEWTON):
                ch.link(nc.vector.tensor_tensor(t, yf, yf, ALU.mult))
                ch.link(nc.vector.scalar_tensor_tensor(out=t, in0=t, scalar=-0.5, in1=v,
                                                       op0=ALU.mult, op1=ALU.mult))
                ch.link(nc.vector.scalar_tensor_tensor(out=yf, in0=t, scalar=1.5, in1=yf,
                                                       op0=ALU.add, op1=ALU.mult))
            return yf

        def q_pair(slot, h):
            return qT[:, slot, :, h:h + 2, :]

        def k_pair(slot, h):
            return kT[:, slot, h:h + 2, :].rearrange("p h (b c) -> p b h c", c=S)

        def by_batch(ap):
            return ap.rearrange("p (b c) -> p b c", c=S).unsqueeze(2).to_broadcast(
                [ap.shape[0], 2 * GT, 2, S])

        def pairs_of(ap):
            return ap.rearrange("p (j c) -> p j c", j=NPAIR)

        block = stack.enter_context(nc.Block())

        @block.sync
        def _(sp):
            rows_in = [x, y_dram]

            def rows(dram, g):
                return dram[bass.ds(g * GTOK, GTOK), :].rearrange("(t p) c -> p t c", p=P)

            def load_rows(ph, g, slot):
                if is_there(g, GROUPS):
                    need(sp, att[ph]["norm_rows"], NORM_LINKS[ph] * (g - 1))
                    sp.dma_start(xin[:, slot], rows(rows_in[ph], g)).then_inc(att[ph][f"x_in{slot}"], 16)

            def load_ctx(g, slot):
                if is_there(g, GROUPS):
                    need(sp, att[CROSS]["cT_ps"], g - 1)
                    need(sp, att[CROSS]["c_lo"], g - 1)
                    sp.dma_start(ctx_raw[:, slot], rows(ctx_in, g)).then_inc(att[CROSS][f"c_in{slot}"], 16)

            def load_res(ph, g, slot):
                if is_there(g, GROUPS):
                    need(sp, att[ph]["tail"], TAIL_LINKS[ph] * GT * (g - 1))
                    sp.dma_start(res[:, slot], rows(rows_in[ph], g)).then_inc(att[ph][f"r_in{slot}"], 16)

            def store(ph, n, slot):
                s = att[ph]
                sp.wait_ge(s["tail"], TAIL_LINKS[ph] * (n + 1))
                if ph == CROSS:
                    sp.dma_start(x1_dram[bass.ds(n * P, P), :], summed[:, slot]).then_inc(s[f"sum_st{slot}"], 16)
                    sp.dma_start(y_dram[bass.ds(n * P, P), :], ln_out[:, slot]).then_inc(s[f"ln_st{slot}"], 16)
                else:
                    sp.dma_start(y1_dram[bass.ds(n * P, P), :], summed[:, slot]).then_inc(s[f"sum_st{slot}"], 16)

            def attention_pass(ph, it):
                for t in range(STEPS):
                    n, g = it * STEPS + t, it * 2 + t // GT
                    if t % GT == 0:
                        load_rows(ph, g + 2, t // GT)
                        if ph == CROSS:
                            load_ctx(g + 2, t // GT)
                        load_res(ph, g + 1, (t // GT + 1) % 2)
                    if type(n) is not int or n > 0:
                        store(ph, n - 1, (t - 1) % 2)

            def all_passes(ph):
                attention_pass(ph, 0)
                with sp.Fori(1, PASSES - 1) as it:
                    attention_pass(ph, it)
                attention_pass(ph, PASSES - 1)
                store(ph, TILES - 1, (TILES - 1) % 2)

            def weights(dst, src, name):
                sp.dma_start(dst.rearrange("p (k c) -> p k c", k=KD),
                             src.rearrange("(k p) c -> p k c", p=P)).then_inc(w_in[name], 16)

            sp.dma_start(eye_f[:], eye).then_inc(eye_in, 16)
            sp.dma_start(flat(kT[:, 0]), Wk).then_inc(w_in["Wk"], 16)
            sp.dma_start(flat(kT[:, 1]), Wv).then_inc(w_in["Wv"], 16)
            weights(q_flat[0], Wq, "Wq")
            sp.dma_start(Wo_raw, Wo.rearrange("(h p) c -> p h c", p=P)).then_inc(w_in["Wo"], 16)
            load_rows(CROSS, 0, 0)
            load_rows(CROSS, 1, 1)
            load_ctx(0, 0)
            load_ctx(1, 1)
            load_res(CROSS, 0, 0)
            sp.dma_start(mask_all, mask.rearrange("(a b) s -> a (b s)", a=1)
                         .to_broadcast([P, B * S])).then_inc(consts_in, 16)
            for dst, src in ((causal_f[:], causal), (cos_t[:], rope[0]), (sin_t[:], rope[1]),
                             (norm_rows_w[0:KD], ln1_w.rearrange("(k p) -> k p", p=P)),
                             (norm_rows_w[KD:2 * KD], ln2_w.rearrange("(k p) -> k p", p=P)),
                             (norm_rows_w[2 * KD:2 * KD + H], qnorm_w.rearrange("(h p) -> h p", p=P)),
                             (norm_rows_w[2 * KD + H:], knorm_w.rearrange("(h p) -> h p", p=P)),
                             (rt_raw[:], router_w.rearrange("(k p) e -> p k e", p=P)),
                             (rt_bias[:], router_bias.rearrange("(a e) -> a e", a=1).to_broadcast([P, E])),
                             (before[:].rearrange("p a b -> p (a b)"), earlier.to_broadcast([P, E * E]))):
                sp.dma_start(dst, src).then_inc(consts_in, 16)
            all_passes(CROSS)

            sp.wait_ge(att[CROSS]["score_ps"], 2 * TILES)
            weights(flat(kT[:, 0])[:, 0:1024], wk, "wk")
            weights(flat(kT[:, 1])[:, 0:1024], wv, "wv")
            weights(q_flat[0], wq, "wq")
            sp.dma_start(Wo_raw, wo.rearrange("(h p) c -> p h c", p=P)).then_inc(w_in["wo"], 16)
            for slot in range(2):
                sp.wait_ge(att[CROSS][f"sum_st{slot}"], 16 * TILES // 2)
                sp.wait_ge(att[CROSS][f"ln_st{slot}"], 16 * TILES // 2)
            load_rows(SELF, 0, 0)
            load_rows(SELF, 1, 1)
            load_res(SELF, 0, 0)
            all_passes(SELF)

            sp.wait_ge(att[SELF]["score_ps"], 2 * TILES)
            for k in range(KD):
                for dst, src, name in ((q_flat[0][:, 0:2048], wg, "wg"), (q_flat[0][:, 2048:4096], wu, "wu")):
                    sp.dma_start(dst.rearrange("p (k e i) -> p k e i", k=KD, e=E)[:, k],
                                 src[:, k * P:(k + 1) * P, :].rearrange("e p i -> p e i")
                                 ).then_inc(w_in[name], 16)
            sp.dma_start(q_flat[1][:, 0:2048].rearrange("p (e c) -> p e c", e=E),
                         wd.rearrange("e p c -> p e c")).then_inc(w_in["wd"], 16)
            for slot in range(2):
                sp.wait_ge(att[SELF][f"sum_st{slot}"], 16 * TILES // 2)
            sp.wait_ge(att[SELF]["pT_ps"], 2 * TILES)

            def chunk_rows(dram, c):
                return dram[bass.ds(c * CTOK, CTOK), :].rearrange("(t p) d -> p t d", p=P)

            def load_chunk(c, slot):
                if is_there(c, CHUNKS):
                    need(sp, ex["norm_rows"], NORM_LINKS[SELF] * (c - 1))
                    need(sp, ex["init"], c - 1)
                    sp.dma_start(yc[:, slot], chunk_rows(y1_dram, c)).then_inc(ex[f"y_in{slot}"], 16)
                    sp.dma_start(xc[:, slot], chunk_rows(x1_dram, c)).then_inc(ex[f"x_in{slot}"], 16)

            def chunk_pair(it):
                for u in range(2):
                    c = it * 2 + u
                    load_chunk(c + 2, u)
                    sp.wait_ge(ex["added"], E * CT * (c + 1))
                    sp.dma_start(chunk_rows(out, c), total[:, u]).then_inc(ex[f"st{u}"], 16)

            load_chunk(0, 0)
            load_chunk(1, 1)
            chunk_pair(0)
            with sp.Fori(1, CHUNKS // 2 - 1) as it:
                chunk_pair(it)
            chunk_pair(CHUNKS // 2 - 1)
            for u in range(2):
                sp.wait_ge(ex[f"st{u}"], 16 * CHUNKS // 2)

        @block.tensor
        def _(pe):
            def mm(dst, lhsT, rhs, start, stop=True):
                return nc.tensor.matmul(dst, lhsT, rhs, start=start, stop=stop, skip_group_check=True)

            def mm3(dst, st, mv, first, final):
                mm(dst, st(0), mv(0), start=first, stop=False)
                mm(dst, st(0), mv(1), start=False, stop=False)
                return mm(dst, st(1), mv(0), start=False, stop=final)

            def fold_weights():
                pe.wait_ge(eye_in, 16)
                for i, (name, dst) in enumerate((("Wk", b_score), ("Wv", b_pv))):
                    pe.wait_ge(w_in[name], 16)
                    for j in range(KVX):
                        last = nc.tensor.transpose(dst[j // 4][:, j % 4 * P:(j % 4 + 1) * P],
                                                   flat(kT[:, i])[:, j * P:(j + 1) * P], eye_f[:])
                        if j % 4 == 3:
                            last.then_inc(pr["wkvT_ps"], 1)

                def transpose_q(j):
                    if j < NPAIR:
                        need(pe, pr["wqT"], j - 1)
                        for i in range(2):
                            for k in range(KD):
                                c = (2 * j + i) * HD
                                last = nc.tensor.transpose(
                                    b_proj[j % 2][:, (2 * i + k) * P:(2 * i + k + 1) * P],
                                    q_flat[0].rearrange("p (k c) -> p k c", k=KD)[:, k, c:c + HD], eye_f[:])
                        last.then_inc(pr["wqT_ps"], 1)

                pe.wait_ge(w_in["Wq"], 16)
                transpose_q(0)
                pe.wait_ge(pr["wkvT"], 4)
                pe.wait_ge(w_in["Wo"], 16)
                for j in range(NPAIR):
                    transpose_q(j + 1)
                    pe.wait_ge(pr["wqT"], j + 1)
                    need(pe, pr["fold_hi"], 2 * j - 3)
                    need(pe, pr["fold_lo"], 2 * j - 3)
                    dst = (b_out, b_misc)[j % 2]
                    for i in range(2):
                        for k in range(KD):
                            c = (2 * i + k) * P
                            last = mm(dst[:, c:c + P], sq[:, j % 2, c:c + P],
                                      fold_T[:, 0, j * P:(j + 1) * P], start=True)
                    last.then_inc(pr["fold_ps"], 1)
                    need(pe, pr["fold_hi"], 2 * j - 2)
                    need(pe, pr["fold_lo"], 2 * j - 2)
                    for i in range(2):
                        last = mm(b_score[j % 2][:, i * D:(i + 1) * D],
                                  fold_T[:, 1, j * P:(j + 1) * P], Wo_raw[:, 2 * j + i, :], start=True)
                    last.then_inc(pr["fold_ps"], 1)

            def transpose_rows(ph, g):
                s = att[ph]
                pe.wait_ge(s["norm_rows"], NORM_LINKS[ph] * (g + 1))
                need(pe, *((s["cT"], g) if ph == CROSS else (s["rq_done"], RQ_LINKS * g)))
                for k in range(KD):
                    for i in range(GT):
                        c = k * GTOK + i * P
                        last = nc.tensor.transpose(b_misc[:, c:c + P], xn[:, i, k * P:(k + 1) * P], eye_f[:])
                last.then_inc(s["hT_ps"], 1)

            def transpose_ctx(g, slot):
                s = att[CROSS]
                pe.wait_ge(s[f"c_in{slot}"], 16 * (g // 2 + 1) if type(g) is int else g_uses(g, slot))
                pe.wait_ge(s["hT_hi"], g + 1)
                pe.wait_ge(s["hT_lo"], g + 1)
                for i in range(GT):
                    last = nc.tensor.transpose(b_misc[:, i * P:(i + 1) * P], ctx_raw[:, slot, i, :], eye_f[:])
                last.then_inc(s["cT_ps"], 1)

            def bank_free(ph, g, j):
                s = att[ph]
                need(pe, s["proj_ev"], PROJ[ph] * g + j - 1)
                if ph == SELF and j < 2:
                    need(pe, s["v_lo"], GT * g + j - 1)

            def project_pair(ph, g, j, w, col):
                bank_free(ph, g, j)
                for i in range(2):
                    for k in range(KD):
                        last = mm3(b_proj[j % 2][:, i * GTOK:(i + 1) * GTOK],
                                   lambda l: w[:, l, k, col + i * HD:col + (i + 1) * HD],
                                   lambda l: hT[:, l, k, :], first=k == 0, final=k == KD - 1)
                last.then_inc(att[ph]["proj_ps"], 1)

            def project_v(g, j, i):
                bank_free(SELF, g, j)
                for k in range(KD):
                    last = mm3(b_proj[j % 2][:], lambda l: hT[:, l, k, i * P:(i + 1) * P],
                               lambda l: W_v[:, l, k, :], first=k == 0, final=k == KD - 1)
                last.then_inc(att[SELF]["proj_ps"], 1)

            def first_work(ph, g):
                s = att[ph]
                pe.wait_ge(s["hT_hi"], g + 1)
                pe.wait_ge(s["hT_lo"], g + 1)
                if ph == CROSS:
                    for j in range(4):
                        project_pair(ph, g, j, W_q, 2 * j * HD)
                else:
                    for j in range(KPAIR):
                        project_pair(ph, g, j, W_k, 2 * j * HD)
                    for j in range(4):
                        project_pair(ph, g, KPAIR + j, W_q, 2 * j * HD)

            def second_work(ph, g):
                s = att[ph]
                if ph == CROSS:
                    for j in range(4, 8):
                        project_pair(ph, g, j, W_q, 2 * j * HD)
                    return
                pe.wait_ge(s["sq_added"], ADDS * g + adds_before(KPAIR - 1))
                for i in range(GT):
                    for a in range(2):
                        last = mm(b_misc[:, i:i + 1], acc_k[:, a, i * P:(i + 1) * P], ones_f[:, 0:1], start=a == 0)
                last.then_inc(s["ssk_ps"], 1)
                for j in range(4, 8):
                    project_pair(ph, g, KPAIR + j, W_q, 2 * j * HD)
                pe.wait_ge(s["rk_done"], RK_LINKS * (g + 1))
                for i in range(GT):
                    last = mm(b_misc[:, GTOK + i * P:GTOK + (i + 1) * P], ones_f[:], diag[:, i, :], start=True)
                last.then_inc(s["rkb_ps"], 1)
                for i in range(GT):
                    project_v(g, KPAIR + NPAIR + i, i)

            def square_sums(g):
                s = att[SELF]
                pe.wait_ge(s["sq_added"], ADDS * (g + 1))
                pe.wait_ge(s["k_scaled"], g + 1)
                for i in range(2 * GT):
                    for r in (0, S):
                        for a in range(2):
                            last = mm(b_misc[r:r + S, i:i + 1], acc_q[:, a, i * S:(i + 1) * S],
                                      ones_f[:, 0:1], start=a == 0)
                last.then_inc(s["ssq_ps"], 1)

            def scores(ph, n, g, t):
                s = att[ph]
                if ph == CROSS:
                    pe.wait_ge(s["proj_ev"], PROJ[ph] * (g + 1))
                    pe.wait_ge(s["cT"], g + 1)
                    pe.wait_ge(s["mask_st"], n + 1)
                else:
                    pe.wait_ge(s["rotated"], ROTS * (g + 1))
                    pe.wait_ge(s["k_scaled"], g + 1)
                slot, base = t // GT % 2, t % GT * P
                for b in range(2):
                    need(pe, s["shifted"], 2 * n + b - 1)
                    dst, tok = b_score[b], base + b * S
                    if ph == CROSS:
                        mm(pairs_of(dst[:]), ones_row[:], mask_row[0:1, t % 2, b * S:(b + 1) * S]
                           .unsqueeze(1).to_broadcast([1, NPAIR, S]), start=True, stop=False)
                    else:
                        mm(pairs_of(dst[:]), eye2_b[:].rearrange("p a c -> p (a c)"),
                           causal_b[:].unsqueeze(1).to_broadcast([S, NPAIR, S]), start=True, stop=False)
                    for j in range(NPAIR):
                        kv = 0 if ph == CROSS else j // 2
                        own = 1 + (slot * 4 + kv) * 2 * GT + tok // S
                        if j < NPAIR - 1:
                            cols, key = j, k_blocks[:, own:K_BLOCKS:K_BLOCKS - 1 - own]
                        else:
                            cols, key = j - 1, k_blocks[:, 0:own + 1:own]
                        last = mm(dst[:, cols * S:(cols + 2) * S].rearrange("p (a c) -> p a c", a=2),
                                  qT[:, slot, tok // S, 2 * j:2 * j + 2, :].rearrange("p h c -> p (h c)"), key,
                                  start=False)
                    last.then_inc(s["score_ps"], 1)

            def transpose_probs(ph, n, t):
                s = att[ph]
                pe.wait_ge(s["probs"], 2 * n + 2)
                need(pe, s["u_hi"], 4 * n)
                need(pe, s["u_lo"], 4 * n)
                for j in range(NPAIR):
                    last = nc.tensor.transpose(b_pv[j // 4][:, j % 4 * P:(j % 4 + 1) * P],
                                               prob[:, t % 2, j].rearrange("p b c -> p (b c)"), eye_f[:])
                    if j % 4 == 3:
                        last.then_inc(s["pT_ps"], 1)

            def prob_v(ph, n, t, half):
                s = att[ph]
                if half == 0:
                    pe.wait_ge(s["pT_hi"], 2 * n + 2)
                    pe.wait_ge(s["pT_lo"], 2 * n + 2)
                    if ph == CROSS:
                        pe.wait_ge(s["c_lo"], n_group(n, t) + 1)
                    else:
                        pe.wait_ge(s["v_lo"], n + 1)
                        pe.wait_ge(s["proj_ev"], PROJ[ph] * (n_group(n, t) + 1) - (GT - 1 - t % GT))
                for b in range(2):
                    if half == 1:
                        pe.wait_ge(s["u_hi"], 4 * n + b + 1)
                        pe.wait_ge(s["u_lo"], 4 * n + b + 1)
                    rows = slice(b * S, (b + 1) * S)
                    if ph == CROSS:
                        last = mm3(b_pv[b][:], lambda l: V[rows, t, l, 0:DV],
                                   lambda l: PT[rows, l, half * 512:(half + 1) * 512], first=True, final=True)
                    else:
                        for a in range(2):
                            c, kv = half * 512 + a * 256, half * 2 + a
                            last = mm3(b_pv[b][:, a * 256:(a + 1) * 256],
                                       lambda l: V[rows, t, l, kv * HD:(kv + 1) * HD],
                                       lambda l: PT[rows, l, c:c + 256], first=True, final=True)
                    last.then_inc(s["pv_ps"], 1)

            def n_group(n, t):
                return n // GT if type(n) is int else group_of[t]

            def project_out(ph, n, half):
                s = att[ph]
                pe.wait_ge(s["u_hi"], 4 * n + 2 * half + 2)
                pe.wait_ge(s["u_lo"], 4 * n + 2 * half + 2)
                if half == 0:
                    need(pe, s["tail"], TAIL_LINKS[ph] * (n - 1) + 2 if type(n) is not int or n > 0 else 0)
                for i in range(NPAIR):
                    h = half * NPAIR + i
                    mm(b_out[:], U[:, half, 0, i, :], W_o[:, h].rearrange("p l c -> p (l c)"),
                       start=h == 0, stop=False)
                    last = mm(b_out[:, 0:D], U[:, half, 1, i, :], W_o[:, h, 0, :], start=False, stop=h == H - 1)
                if half == 1:
                    last.then_inc(s["out_ps"], 1)

            group_of = {}
            uses_of = {}

            def g_uses(g, slot):
                return uses_of[slot]

            def step(ph, it, t):
                n = it * STEPS + t
                gs = it * 2
                group_of[t] = gs + t // GT
                transpose_probs(ph, n, t)
                ahead = gs + (t // GT + 2 if t % 2 else t // GT + 1)
                if t % 2:
                    if is_there(ahead, GROUPS):
                        transpose_rows(ph, ahead)
                elif ph == CROSS and is_there(ahead, GROUPS):
                    slot = (t // GT + 1) % 2
                    uses_of[slot] = (it + (t // GT + 1) // 2) * 16 + 16
                    transpose_ctx(ahead, slot)
                if is_there(n + 1, TILES):
                    scores(ph, n + 1, gs + (t + 1) // GT, (t + 1) % STEPS)
                if is_there(ahead, GROUPS):
                    (first_work if t % 2 else second_work)(ph, ahead)
                prob_v(ph, n, t, 0)
                if type(n) is not int or n > 0:
                    project_out(ph, n - 1, 1)
                prob_v(ph, n, t, 1)
                project_out(ph, n, 0)
                if ph == SELF and t % 2 == 0 and is_there(ahead, GROUPS):
                    square_sums(ahead)

            def attention(ph):
                transpose_rows(ph, 0)
                if ph == CROSS:
                    transpose_ctx(0, 0)
                first_work(ph, 0)
                second_work(ph, 0)
                if ph == SELF:
                    square_sums(0)
                transpose_rows(ph, 1)
                first_work(ph, 1)
                scores(ph, 0, 0, 0)
                for t in range(STEPS):
                    step(ph, 0, t)
                with pe.Fori(1, PASSES - 1) as it:
                    for t in range(STEPS):
                        step(ph, it, t)
                for t in range(STEPS):
                    step(ph, PASSES - 1, t)
                project_out(ph, TILES - 1, 1)

            fold_weights()
            pe.wait_ge(consts_in, N_CONSTS)
            nc.tensor.transpose(b_proj[0][:, 0:N_NORM_W], norm_rows_w[:], eye_f[0:N_NORM_W, 0:N_NORM_W]
                                ).then_inc(pr["normT_ps"], 1)
            pe.wait_ge(pr["normT"], 1)
            pe.wait_ge(pr["fold_hi"], 2 * NPAIR)
            pe.wait_ge(pr["fold_lo"], 2 * NPAIR)
            pe.wait_ge(pr["consts"], 1)
            attention(CROSS)
            pe.wait_ge(pr["hi_s"], 7)
            pe.wait_ge(pr["lo_s"], 6)
            pe.wait_ge(pr["lo_wo"], 1)
            attention(SELF)

            pe.wait_ge(pr["hi_e"], 5)
            pe.wait_ge(pr["lo_e"], 4)
            pe.wait_ge(pr["lo_wd"], 1)
            pe.wait_ge(pr["rt_w"], 1)
            t_banks = (b_out, b_misc)

            def transpose_chunk(c):
                pe.wait_ge(ex["norm_rows"], NORM_LINKS[SELF] * (c + 1))
                need(pe, ex["rt_exp"], c)
                need(pe, ex["h_lo"], c)
                for k in range(KD):
                    for i in range(CT):
                        last = nc.tensor.transpose(t_banks[k][:, i * P:(i + 1) * P],
                                                   yn[:, i, k * P:(k + 1) * P], eye_f[:])
                last.then_inc(ex["T_ps"], 1)

            def router(c, u):
                pe.wait_ge(ex["h_full"], c + 1)
                pe.wait_ge(ex["h_hi"], c + 1)
                pe.wait_ge(ex["h_lo"], c + 1)
                for i in range(CT):
                    for k in range(KD):
                        last = mm(b_out[:, i * E:(i + 1) * E], h_full[:, u, k, i * P:(i + 1) * P],
                                  rt_w[:, k, :], start=k == 0, stop=k == KD - 1)
                last.then_inc(ex["rt_ps"], 1)

            def gate_up(c, u, e):
                i = c * E + e
                pe.wait_ge(ex["h_hi"], c + 1)
                pe.wait_ge(ex["h_lo"], c + 1)
                need(pe, ex["gated"], i - 1)
                for k in range(KD):
                    last = mm3(b_score[e % 2][:], lambda l: W_g[:, l, k, e * FI:(e + 1) * FI],
                               lambda l: h2T[:, u, l, k, :], first=k == 0, final=k == KD - 1)
                last.then_inc(ex["gate_ps"], 1)
                need(pe, ex["act"], i - 1)
                for k in range(KD):
                    last = mm3(b_pv[e % 2][:], lambda l: W_u[:, l, k, e * FI:(e + 1) * FI],
                               lambda l: h2T[:, u, l, k, :], first=k == 0, final=k == KD - 1)
                last.then_inc(ex["up_ps"], 1)

            def down(i, e):
                pe.wait_ge(ex["a_hi"], i + 1)
                pe.wait_ge(ex["a_lo"], i + 1)
                for b in range(2):
                    need(pe, ex["added"], CT * i - 2 + 2 * b if type(i) is not int or i > 0 else 0)
                    for a in range(2):
                        c = (2 * b + a) * P
                        last = mm3(b_proj[b][:, a * D:(a + 1) * D], lambda l: actT[:, e % 2, l, c:c + P],
                                   lambda l: W_d[:, l, e, :], first=True, final=True)
                    last.then_inc(ex["down_ps"], 1)

            def chunk_pair(it):
                for u in range(2):
                    c = it * 2 + u
                    for e in range(E):
                        gate_up(c, u, e)
                        i = c * E + e
                        if type(i) is not int or i > 0:
                            down(i - 1, (e - 1) % E)
                        if e == 3 and is_there(c + 1, CHUNKS):
                            transpose_chunk(c + 1)
                        if e == 5 and is_there(c + 1, CHUNKS):
                            router(c + 1, 1 - u)

            transpose_chunk(0)
            router(0, 0)
            chunk_pair(0)
            with pe.Fori(1, CHUNKS // 2 - 1) as it:
                chunk_pair(it)
            chunk_pair(CHUNKS // 2 - 1)
            down(CHUNKS * E - 1, E - 1)

        @block.scalar
        def _(act):
            def copy(dst, src, scale=1.0):
                return nc.scalar.activation(dst, src, ACT.Copy, scale=scale)

            def fold_weights():
                for i in range(4):
                    act.wait_ge(pr["wkvT_ps"], i + 1)
                    copy(fold_T[:, i // 2, i % 2 * 512:(i % 2 + 1) * 512], (b_score, b_pv)[i // 2][i % 2][:]).then_inc(pr["wkvT"], 1)

                def split_high(j):
                    act.wait_ge(pr["fold_ps"], 2 * j + 1)
                    copy(W_q[:, 0, :, 2 * j * HD:2 * (j + 1) * HD].rearrange("p k (h c) -> p h k c", h=2),
                         (b_out, b_misc)[j % 2][:].rearrange("p (h k c) -> p h k c", h=2, k=KD)
                         ).then_inc(pr["fold_hi"], 1)
                    act.wait_ge(pr["fold_ps"], 2 * j + 2)
                    copy(W_o[:, 2 * j:2 * j + 2, 0, :],
                         b_score[j % 2][:].rearrange("p (h c) -> p h c", h=2)).then_inc(pr["fold_hi"], 1)

                for j in range(NPAIR + 1):
                    if j < NPAIR:
                        act.wait_ge(pr["wqT_ps"], j + 1)
                        need(act, pr["fold_ps"], 2 * j - 3)
                        copy(sq[:, j % 2], b_proj[j % 2][:]).then_inc(pr["wqT"], 1)
                    if j > 0:
                        split_high(j - 1)
                act.wait_ge(pr["normT_ps"], 1)
                copy(norm_w[:], b_proj[0][:, 0:N_NORM_W]).then_inc(pr["normT"], 1)

            def rows_high(ph, g):
                s = att[ph]
                act.wait_ge(s["hT_ps"], g + 1)
                need(act, s["proj_ps"], PROJ[ph] * g)
                copy(hT[:, 0], b_misc[:].rearrange("p (k c) -> p k c", k=KD)).then_inc(s["hT_hi"], 1)

            def stage_mask(n, slot):
                s = att[CROSS]
                if is_there(n, TILES):
                    need(act, s["score_ps"], 2 * (n - 1))
                    nc.scalar.activation(mask_row[0:1, slot, :], mask_all[0:1, bass.ds(n * P, P)], ACT.Copy,
                                         scale=-MASKED, bias=MASKED).then_inc(s["mask_st"], 1)

            def ctx_copy(g, slot):
                s = att[CROSS]
                act.wait_ge(s["cT_ps"], g + 1)
                need(act, s["pv_ps"], 4 * GT * (g - 1))
                copy(V[:, GT * slot:GT * (slot + 1), 0, 0:DV], ctx_raw[:, slot]).then_inc(s["c_hi"], 1)
                act.wait_ge(s["cT_ps"], g + 1)
                copy(kT[:, slot, 0, :], b_misc[:, 0:GTOK]).then_inc(s["cT"], 1)

            def read_pair(ph, g, slot, j):
                s = att[ph]
                act.wait_ge(s["proj_ps"], PROJ[ph] * g + j + 1)
                src = b_proj[j % 2][:]
                if ph == CROSS:
                    for i in range(2):
                        last = copy(qT[:, slot, :, 2 * j + i, :],
                                    src[:, i * GTOK:(i + 1) * GTOK].rearrange("p (b c) -> p b c", c=S))
                    last.then_inc(s["proj_ev"], 1)
                    return
                is_k = j < KPAIR
                h = 2 * j if is_k else 2 * (j - KPAIR)
                for i in range(2):
                    dst = (k_pair if is_k else q_pair)(slot, h)[:, :, i, :]
                    col = (H if is_k else 0) + h + i
                    copy(dst, src[:, i * GTOK:(i + 1) * GTOK].rearrange("p (b c) -> p b c", c=S),
                         scale=qk_w[:, col:col + 1])
                need(act, s["sq_added"], ADDS * g + (adds_before(j - 2) if j > 1 else j - 1))
                nc.scalar.activation(sq[:, j % 2], src, ACT.Square).then_inc(s["proj_ev"], 1)

            def read_v(g, gslot, i):
                s = att[SELF]
                j = KPAIR + NPAIR + i
                act.wait_ge(s["proj_ps"], PROJ[SELF] * g + j + 1)
                copy(V[:, GT * gslot + i, 0, :], b_proj[j % 2][:]).then_inc(s["proj_ev"], 1)

            def exps(ph, n, t, b):
                s = att[ph]
                act.wait_ge(s["shifted"], 2 * n + b + 1)
                scale = SCORE_SCALE
                if ph == SELF:
                    i = t % GT * 2 + b
                    if b == 0:
                        act.wait_ge(s["rq_done"], RQ_LINKS * (group_of[t] + 1))
                    scale = q_factor[:, t // GT, i:i + 1]
                p = prob[:, t % 2, :, b, :]
                nc.scalar.activation(p, p, ACT.Exp, scale=scale).then_inc(s["expd"], 1)

            def probs_high(ph, n):
                s = att[ph]
                for i in range(2):
                    act.wait_ge(s["pT_ps"], 2 * n + i + 1)
                    copy(PT[:, 0, i * 512:(i + 1) * 512], b_pv[i][:]).then_inc(s["pT_hi"], 1)

            def u_high(ph, n, half):
                s = att[ph]
                for b in range(2):
                    act.wait_ge(s["pv_ps"], 4 * n + 2 * half + b + 1)
                    copy(U[:, half, 0, :, b * S:(b + 1) * S],
                         b_pv[b][:].rearrange("p (h c) -> p h c", h=NPAIR)).then_inc(s["u_hi"], 1)

            group_of = {}

            def work(ph, g, slot, second, between=()):
                if ph == CROSS:
                    js = range(4, 8) if second else range(4)
                else:
                    js = range(KPAIR + 4, KPAIR + NPAIR) if second else range(KPAIR + 4)
                between = list(between)
                for j in js:
                    if between:
                        between.pop(0)()
                    read_pair(ph, g, slot, j)
                if ph == SELF and second:
                    for i in range(GT):
                        read_v(g, slot, i)

            def step(ph, it, t):
                n, gs = it * STEPS + t, it * 2
                probs_high(ph, n)
                ahead = gs + (t // GT + 2 if t % 2 else t // GT + 1)
                slot = (t // GT + (2 if t % 2 else 1)) % 2
                there = is_there(ahead, GROUPS)
                if there and t % 2:
                    rows_high(ph, ahead)
                elif there and ph == CROSS:
                    ctx_copy(ahead, slot)
                if ph == CROSS:
                    stage_mask(n + 2, t % 2)
                t1 = (t + 1) % STEPS
                group_of[t1] = gs + (t + 1) // GT
                between = [lambda b=b: exps(ph, n + 1, t1, b) for b in range(2)] if is_there(n + 1, TILES) else []
                if there:
                    work(ph, ahead, slot, t % 2 == 0, between)
                else:
                    for f in between:
                        f()
                u_high(ph, n, 0)
                u_high(ph, n, 1)

            def attention(ph):
                rows_high(ph, 0)
                if ph == CROSS:
                    act.wait_ge(consts_in, N_CONSTS)
                    stage_mask(0, 0)
                    stage_mask(1, 1)
                    ctx_copy(0, 0)
                work(ph, 0, 0, False)
                work(ph, 0, 0, True)
                rows_high(ph, 1)
                work(ph, 1, 1, False)
                group_of[0] = 0
                for b in range(2):
                    exps(ph, 0, 0, b)
                for t in range(STEPS):
                    step(ph, 0, t)
                with act.Fori(1, PASSES - 1) as it:
                    for t in range(STEPS):
                        step(ph, it, t)
                for t in range(STEPS):
                    step(ph, PASSES - 1, t)

            fold_weights()
            attention(CROSS)

            act.wait_ge(pr["normT"], 1)
            for name, dst, src in (("wk", W_k, flat(kT[:, 0])), ("wq", W_q, q_flat[0]), ("wv", W_v, flat(kT[:, 1]))):
                act.wait_ge(w_in[name], 16)
                src = src.rearrange("p (k c) -> p k c", k=KD)
                for k in range(KD):
                    copy(dst[:, 0, k, :], src[:, k, :], scale=ln_w[:, 0, k:k + 1]).then_inc(pr["hi_s"], 1)
            act.wait_ge(w_in["wo"], 16)
            act.wait_ge(att[CROSS]["out_ps"], TILES)
            copy(W_o[:, :, 0, :], Wo_raw).then_inc(pr["hi_s"], 1)
            attention(SELF)

            for name, dst, src in (("wg", W_g, q_flat[0][:, 0:2048]), ("wu", W_u, q_flat[0][:, 2048:4096])):
                act.wait_ge(w_in[name], 32)
                src = src.rearrange("p (k c) -> p k c", k=KD)
                for k in range(KD):
                    copy(dst[:, 0, k, :], src[:, k, :], scale=ln_w[:, 1, k:k + 1]).then_inc(pr["hi_e"], 1)
            act.wait_ge(w_in["wd"], 16)
            act.wait_ge(att[SELF]["out_ps"], TILES)
            copy(W_d[:, 0], q_flat[1][:, 0:2048].rearrange("p (e c) -> p e c", e=E)).then_inc(pr["hi_e"], 1)

            def chunk_rows(c, u):
                act.wait_ge(ex["T_ps"], c + 1)
                for k, bank in enumerate((b_out, b_misc)):
                    last = copy(h_full[:, u, k, :], bank[:])
                last.then_inc(ex["h_full"], 1)
                for k, bank in enumerate((b_out, b_misc)):
                    last = copy(h2T[:, u, 0, k, :], bank[:])
                last.then_inc(ex["h_hi"], 1)

            def route_exp(c):
                act.wait_ge(ex["rt_ps"], c + 1)
                need(act, ex["routed"], ROUTE_LINKS * c)
                nc.scalar.activation(route[:, 0].rearrange("p t e -> p (t e)"), b_out[:, 0:CT * E], ACT.Exp,
                                     scale=-1.0).then_inc(ex["rt_exp"], 1)

            def chunk_pair(it):
                for u in range(2):
                    c = it * 2 + u
                    for e in range(E):
                        i = c * E + e
                        act.wait_ge(ex["gate_ps"], i + 1)
                        need(act, ex["gated"], i - 1)
                        nc.scalar.activation(th[:, e % 2], b_score[e % 2][:], ACT.Tanh, scale=0.5
                                             ).then_inc(ex["tanh"], 1)
                        act.wait_ge(ex["act"], i + 1)
                        need(act, ex["down_ps"], 2 * (i - 1))
                        copy(actT[:, e % 2, 0], act_f[:, e % 2]).then_inc(ex["a_hi"], 1)
                        if e == 3 and is_there(c + 1, CHUNKS):
                            chunk_rows(c + 1, 1 - u)
                        if e == 5 and is_there(c + 1, CHUNKS):
                            route_exp(c + 1)

            act.wait_ge(pr["lo_e"], 4)
            act.wait_ge(pr["lo_wd"], 1)
            chunk_rows(0, 0)
            route_exp(0)
            chunk_pair(0)
            with act.Fori(1, CHUNKS // 2 - 1) as it:
                chunk_pair(it)
            chunk_pair(CHUNKS // 2 - 1)

        @block.vector
        def _(dve):
            tt, ts = nc.vector.tensor_tensor, nc.vector.tensor_scalar

            def low(dst, src, high):
                return tt(dst, src, high, ALU.subtract)

            def constants():
                nc.vector.memset(ones_f[:], 1.0)
                for i in (0, K_BLOCKS - 1):
                    nc.vector.memset(k_blocks[:, i, :], 0.0)
                nc.vector.memset(ones_row[:], 1.0)
                dve.wait_ge(eye_in, 16)
                for i in range(2):
                    nc.vector.tensor_copy(eye2_b[:, i, :], eye_f[0:S, 0:S])
                dve.wait_ge(consts_in, N_CONSTS)
                nc.vector.tensor_copy(causal_b[:], causal_f[:])
                nc.vector.reduce_max(any_valid[:], mask_all.rearrange("p (b s) -> p b s", b=B), AX_X
                                     ).then_inc(pr["consts"], 1)

            def fold_weights():
                for j in range(NPAIR):
                    dve.wait_ge(pr["fold_hi"], 2 * j + 1)
                    cols = slice(2 * j * HD, 2 * (j + 1) * HD)
                    for i in range(2):
                        hc = slice((2 * j + i) * HD, (2 * j + i + 1) * HD)
                        last = low(W_q[:, 1, :, hc],
                                   (b_out, b_misc)[j % 2][:, i * D:(i + 1) * D].rearrange("p (k c) -> p k c", k=KD),
                                   W_q[:, 0, :, hc])
                    last.then_inc(pr["fold_lo"], 1)
                    dve.wait_ge(pr["fold_hi"], 2 * j + 2)
                    low(W_o[:, 2 * j:2 * j + 2, 1, :], b_score[j % 2][:].rearrange("p (h c) -> p h c", h=2),
                        W_o[:, 2 * j:2 * j + 2, 0, :]).then_inc(pr["fold_lo"], 1)

            def norm_rows(s, run, n, rows_of, dst_of, subtract_mean):
                ch = Chain(dve, s["norm_rows"], run, NORM_LINKS[CROSS if subtract_mean else SELF])
                for i in range(n - 1):
                    nc.vector.bn_stats(stat6[:, i, :], rows_of(i))
                ch.link(nc.vector.bn_stats(stat6[:, n - 1, :], rows_of(n - 1)))
                dve.nop(nofuse=True)
                for i in range(n - 1):
                    nc.vector.bn_aggr(stat[:, i, :], stat6[:, i, :])
                ch.link(nc.vector.bn_aggr(stat[:, n - 1, :], stat6[:, n - 1, :]))
                mean, var = stat[:, 0:n, 0], stat[:, 0:n, 1]
                if subtract_mean:
                    r = rsqrt(ch, var, rs_v, rs_t, rs_y, n, LN_EPS)
                else:
                    ch.link(tt(rs_t[:, 0:n], mean, mean, ALU.mult))
                    ch.link(tt(rs_v[:, 0:n], rs_t[:, 0:n], var, ALU.add))
                    r = rsqrt(ch, rs_v[:, 0:n], rs_v, rs_t, rs_y, n, RMS_EPS)
                for i in range(n):
                    if subtract_mean:
                        last = ts(dst_of(i), rows_of(i), stat[:, i, 0:1], r[:, i:i + 1], ALU.subtract, ALU.mult)
                    else:
                        last = ts(dst_of(i), rows_of(i), r[:, i:i + 1], None, ALU.mult)
                ch.last(last)

            def norm_group(ph, g, slot, uses):
                s = att[ph]
                dve.wait_ge(s[f"x_in{slot}"], 16 * uses)
                need(dve, s["hT_ps"], g)
                norm_rows(s, g, GT, lambda i: xin[:, slot, i, :], lambda i: xn[:, i, :], ph == CROSS)

            def rows_low(ph, g):
                s = att[ph]
                dve.wait_ge(s["hT_hi"], g + 1)
                low(hT[:, 1], b_misc[:].rearrange("p (k c) -> p k c", k=KD), hT[:, 0]).then_inc(s["hT_lo"], 1)

            def softmax_shift(ph, n, t):
                s = att[ph]
                for b in range(2):
                    dve.wait_ge(s["score_ps"], 2 * n + b + 1)
                    m, src = mx[:, t % 2, b, :], pairs_of(b_score[b][:])
                    nc.vector.reduce_max(m, src, AX_X).then_inc(s["row_max"], 1)
                    dve.wait_ge(s["row_max"], 2 * n + b + 1)
                    tt(prob[:, t % 2, :, b, :], src, m.unsqueeze(2).to_broadcast([P, NPAIR, S]),
                       ALU.subtract).then_inc(s["shifted"], 1)

            def softmax_sum(ph, n, t):
                s = att[ph]
                ch = Chain(dve, s["row_sum"], n, SUM_LINKS[ph])
                for b in range(2):
                    dve.wait_ge(s["expd"], 2 * n + b + 1)
                    last = nc.vector.reduce_sum(sm[:, t % 2, b, :], prob[:, t % 2, :, b, :], AX_X)
                ch.link(last)
                r = sm[:, t % 2]
                if ph == CROSS:
                    ch.link(nc.vector.reciprocal(r, r))
                    ch.last(tt(r, r, any_valid[:, bass.ds(n * 2, 2)].unsqueeze(2).to_broadcast([P, 2, NPAIR]),
                               ALU.mult))
                else:
                    ch.last(nc.vector.reciprocal(r, r))

            def probs_low(ph, n):
                s = att[ph]
                for i in range(2):
                    dve.wait_ge(s["pT_hi"], 2 * n + i + 1)
                    low(PT[:, 1, i * 512:(i + 1) * 512], b_pv[i][:], PT[:, 0, i * 512:(i + 1) * 512]
                        ).then_inc(s["pT_lo"], 1)

            def u_low(ph, n, half):
                s = att[ph]
                for b in range(2):
                    dve.wait_ge(s["u_hi"], 4 * n + 2 * half + b + 1)
                    c = slice(b * S, (b + 1) * S)
                    low(U[:, half, 1, :, c], b_pv[b][:].rearrange("p (h c) -> p h c", h=NPAIR),
                        U[:, half, 0, :, c]).then_inc(s["u_lo"], 1)

            def tail_sum(ph, n, t, it):
                s = att[ph]
                slot = t // GT % 2
                ch = Chain(dve, s["tail"], n, TAIL_LINKS[ph])
                dve.wait_ge(s["out_ps"], n + 1)
                dve.wait_ge(s[f"r_in{slot}"], 16 * (it + 1))
                need(dve, s[f"sum_st{t % 2}"], 16 * (it * 2 + t // 2))
                ch.link(tt(half_sum[:], b_out[:, 0:D], res[:, slot, t % GT, :], ALU.add))
                total_ = tt(summed[:, t % 2, :], b_out[:, D:2 * D], half_sum[:], ALU.add)
                if ph == SELF:
                    ch.last(total_)
                else:
                    ch.link(total_)
                return ch

            def tail_norm(ch, t, it):
                s = att[CROSS]
                ch.link(nc.vector.bn_stats(tstat6[:], summed[:, t % 2, :]))
                dve.nop(nofuse=True)
                ch.link(nc.vector.bn_aggr(tstat[:], tstat6[:]))
                r = rsqrt(ch, tstat[:, 1:2], ts_v, ts_t, ts_y, 1, LN_EPS)
                need(dve, s[f"ln_st{t % 2}"], 16 * (it * 2 + t // 2))
                ch.last(ts(ln_out[:, t % 2, :], summed[:, t % 2, :], tstat[:, 0:1], r, ALU.subtract, ALU.mult))

            def crosses(g, slot, js):
                s = att[SELF]
                for j in js:
                    dve.wait_ge(s["proj_ev"], PROJ[SELF] * g + j + 1)
                    need(dve, s["rotated"], ROTS * g + j - 1)
                    h = 2 * j if j < KPAIR else 2 * (j - KPAIR)
                    src = (k_pair if j < KPAIR else q_pair)(slot, h)
                    for a, b in ((0, HALF), (HALF, 0)):
                        last = tt(rot[a:a + HALF, j % 2].rearrange("p (b h c) -> p b h c", h=2, c=S),
                                  src[b:b + HALF], by_batch(sin_t[b:b + HALF]), ALU.mult)
                    last.then_inc(s["cross"], 1)

            def k_factors(g):
                s = att[SELF]
                ch = Chain(dve, s["rk_done"], g, RK_LINKS)
                dve.wait_ge(s["ssk_ps"], g + 1)
                r = rsqrt(ch, b_misc[:, 0:GT], ts_v, ts_t, ts_y, GT, RMS_EPS, 1.0 / (KVS * HD))
                for i in range(GT):
                    last = ts(diag[:, i, :], eye_f[:], r[:, i:i + 1], None, ALU.mult)
                ch.last(last)

            def k_scale(g, slot):
                s = att[SELF]
                dve.wait_ge(s["rkb_ps"], g + 1)
                dve.wait_ge(s["rotated"], ROTS * g + KPAIR)
                tt(kT[:, slot], kT[:, slot], b_misc[:, GTOK:2 * GTOK].unsqueeze(1).to_broadcast([P, KVS, GTOK]),
                   ALU.mult).then_inc(s["k_scaled"], 1)

            def q_factors(g, slot):
                s = att[SELF]
                ch = Chain(dve, s["rq_done"], g, RQ_LINKS)
                dve.wait_ge(s["ssq_ps"], g + 1)
                r = rsqrt(ch, b_misc[:, 0:2 * GT], ts_v, ts_t, ts_y, 2 * GT, RMS_EPS, 1.0 / (H * HD))
                ch.last(ts(q_factor[:, slot, :], r, SCORE_SCALE, None, ALU.mult))

            def v_low(g, gslot):
                s = att[SELF]
                for i in range(GT):
                    j = KPAIR + NPAIR + i
                    dve.wait_ge(s["proj_ev"], PROJ[SELF] * g + j + 1)
                    low(V[:, GT * gslot + i, 1, :], b_proj[j % 2][:], V[:, GT * gslot + i, 0, :]
                        ).then_inc(s["v_lo"], 1)

            def step(ph, it, t):
                n, gs = it * STEPS + t, it * 2
                ahead = gs + (t // GT + 2 if t % 2 else t // GT + 1)
                slot = (t // GT + (2 if t % 2 else 1)) % 2
                there, more = is_there(ahead, GROUPS), is_there(n + 1, TILES)
                if ph == SELF and t % 2 and is_there(gs + t // GT + 1, GROUPS):
                    q_factors(gs + t // GT + 1, (t // GT + 1) % 2)
                probs_low(ph, n)
                if there and t % 2:
                    rows_low(ph, ahead)
                if more:
                    softmax_shift(ph, n + 1, (t + 1) % STEPS)
                if ph == SELF and there:
                    if t % 2:
                        crosses(ahead, slot, range(0, 1))
                    else:
                        k_factors(ahead)
                        crosses(ahead, slot, range(6, 7))
                if more:
                    softmax_sum(ph, n + 1, (t + 1) % STEPS)
                if ph == SELF and there:
                    if t % 2:
                        crosses(ahead, slot, range(1, 5))
                    else:
                        crosses(ahead, slot, range(7, 10))
                        k_scale(ahead, slot)
                        v_low(ahead, slot)
                if t % 2 == 0 and is_there(gs + t // GT + 2, GROUPS):
                    norm_group(ph, gs + t // GT + 2, t // GT % 2, it + 2)
                u_low(ph, n, 0)
                if ph == SELF and there and t % 2:
                    crosses(ahead, slot, range(5, 6))
                before_ = (t - 1) % STEPS, it - (1 if t == 0 else 0)
                ch = None
                if type(n) is not int or n > 0:
                    ch = tail_sum(ph, n - 1, *before_)
                u_low(ph, n, 1)
                if ch and ph == CROSS:
                    tail_norm(ch, *before_)

            def attention(ph):
                norm_group(ph, 0, 0, 1)
                rows_low(ph, 0)
                norm_group(ph, 1, 1, 1)
                if ph == SELF:
                    crosses(0, 0, range(0, 6))
                    k_factors(0)
                    crosses(0, 0, range(6, 10))
                    k_scale(0, 0)
                    v_low(0, 0)
                    q_factors(0, 0)
                rows_low(ph, 1)
                if ph == SELF:
                    crosses(1, 1, range(0, 6))
                softmax_shift(ph, 0, 0)
                softmax_sum(ph, 0, 0)
                for t in range(STEPS):
                    step(ph, 0, t)
                with dve.Fori(1, PASSES - 1) as it:
                    for t in range(STEPS):
                        step(ph, it, t)
                for t in range(STEPS):
                    step(ph, PASSES - 1, t)
                ch = tail_sum(ph, TILES - 1, STEPS - 1, PASSES - 1)
                if ph == CROSS:
                    tail_norm(ch, STEPS - 1, PASSES - 1)

            constants()
            fold_weights()
            dve.wait_ge(pr["consts"], 1)
            attention(CROSS)

            for a, (dst, src) in enumerate(((W_k, flat(kT[:, 0])), (W_q, q_flat[0]), (W_v, flat(kT[:, 1])))):
                src = src.rearrange("p (k c) -> p k c", k=KD)
                for k in range(KD):
                    dve.wait_ge(pr["hi_s"], 2 * a + k + 1)
                    nc.vector.scalar_tensor_tensor(out=dst[:, 1, k, :], in0=src[:, k, :], scalar=ln_w[:, 0, k:k + 1],
                                                   in1=dst[:, 0, k, :], op0=ALU.mult, op1=ALU.subtract
                                                   ).then_inc(pr["lo_s"], 1)
            attention(SELF)

            for k in range(KD):
                last = ts(rt_w[:, k, :], rt_raw[:, k, :], ln_w[:, 1, k:k + 1], None, ALU.mult)
            last.then_inc(pr["rt_w"], 1)
            for a, (dst, src) in enumerate(((W_g, q_flat[0][:, 0:2048]), (W_u, q_flat[0][:, 2048:4096]))):
                src = src.rearrange("p (k c) -> p k c", k=KD)
                for k in range(KD):
                    dve.wait_ge(pr["hi_e"], 2 * a + k + 1)
                    nc.vector.scalar_tensor_tensor(out=dst[:, 1, k, :], in0=src[:, k, :], scalar=ln_w[:, 1, k:k + 1],
                                                   in1=dst[:, 0, k, :], op0=ALU.mult, op1=ALU.subtract
                                                   ).then_inc(pr["lo_e"], 1)

            def chunk_norm(c, u, uses):
                dve.wait_ge(ex[f"y_in{u}"], 16 * uses)
                need(dve, ex["T_ps"], c)
                norm_rows(ex, c, CT, lambda i: yc[:, u, i, :], lambda i: yn[:, i, :], False)

            def chunk_low(c, u):
                dve.wait_ge(ex["h_hi"], c + 1)
                for k, bank in enumerate((b_out, b_misc)):
                    last = low(h2T[:, u, 1, k, :], bank[:], h2T[:, u, 0, k, :])
                last.then_inc(ex["h_lo"], 1)

            def top_experts(c, u):
                ch = Chain(dve, ex["routed"], c, ROUTE_LINKS)
                dve.wait_ge(ex["rt_exp"], c + 1)
                sig, val, cnt, picked = (route[:, i] for i in range(4))
                sums, inv = route[:, 4, :, 0], route[:, 4, :, 1]
                gt, eq = (rank3[:, i].rearrange("p t (e f) -> p t e f", e=E) for i in range(2))
                ch.link(ts(sig, sig, 1.0, None, ALU.add))
                ch.link(nc.vector.reciprocal(sig, sig))
                ch.link(tt(val, sig, rt_bias[:].unsqueeze(1).to_broadcast([P, CT, E]), ALU.add))
                other = val.unsqueeze(2).to_broadcast([P, CT, E, E])
                own = val.unsqueeze(3).to_broadcast([P, CT, E, E])
                ch.link(tt(gt, other, own, ALU.is_gt))
                ch.link(tt(eq, other, own, ALU.is_equal))
                ch.link(tt(eq, eq, before[:].unsqueeze(1).to_broadcast([P, CT, E, E]), ALU.mult))
                ch.link(tt(gt, gt, eq, ALU.add))
                ch.link(nc.vector.reduce_sum(cnt, gt, AX_X))
                ch.link(nc.vector.scalar_tensor_tensor(out=picked, in0=cnt, scalar=float(TOPK), in1=sig,
                                                       op0=ALU.is_lt, op1=ALU.mult))
                ch.link(nc.vector.reduce_sum(sums, picked, AX_X))
                ch.link(nc.vector.reciprocal(inv, sums))
                ch.last(nc.vector.scalar_tensor_tensor(out=comb[:, u], in0=picked, scalar=0.5,
                                                       in1=inv.unsqueeze(2).to_broadcast([P, CT, E]),
                                                       op0=ALU.mult, op1=ALU.mult))

            def add_expert(i, u, e):
                for b in range(2):
                    dve.wait_ge(ex["down_ps"], 2 * i + b + 1)
                    for a in range(2):
                        tile = 2 * b + a
                        if e > 0:
                            dve.wait_ge(ex["added"], CT * (i - 1) + tile + 1)
                        nc.vector.scalar_tensor_tensor(
                            out=total[:, u, tile, :], in0=b_proj[b][:, a * D:(a + 1) * D],
                            scalar=comb[:, u, tile, e:e + 1], in1=total[:, u, tile, :],
                            op0=ALU.mult, op1=ALU.add).then_inc(ex["added"], 1)

            def chunk_pair(it):
                for u in range(2):
                    c = it * 2 + u
                    for e in range(E):
                        i = c * E + e
                        dve.wait_ge(ex["tanh"], i + 1)
                        nc.vector.scalar_tensor_tensor(out=gated[:, e % 2], in0=th[:, e % 2], scalar=1.0,
                                                       in1=b_score[e % 2][:], op0=ALU.add, op1=ALU.mult
                                                       ).then_inc(ex["gated"], 1)
                        dve.wait_ge(ex["gated"], i + 1)
                        dve.wait_ge(ex["up_ps"], i + 1)
                        need(dve, ex["a_lo"], i - 1)
                        tt(act_f[:, e % 2], gated[:, e % 2], b_pv[e % 2][:], ALU.mult).then_inc(ex["act"], 1)
                        if type(i) is not int or i > 0:
                            if e == 1:
                                dve.wait_ge(ex["init"], c + 1)
                                dve.wait_ge(ex["routed"], ROUTE_LINKS * (c + 1))
                            add_expert(i - 1, u if e else 1 - u, (e - 1) % E)
                        if e == 1 and is_there(c + 1, CHUNKS):
                            chunk_norm(c + 1, 1 - u, it + 1 + (1 if u else 0))
                        if e == 3 and is_there(c + 1, CHUNKS):
                            chunk_low(c + 1, 1 - u)
                        if e == 5 and is_there(c + 1, CHUNKS):
                            top_experts(c + 1, 1 - u)

            dve.wait_ge(pr["hi_e"], 5)
            dve.wait_ge(pr["lo_e"], 4)
            dve.wait_ge(pr["lo_wd"], 1)
            chunk_norm(0, 0, 1)
            chunk_low(0, 0)
            top_experts(0, 0)
            chunk_pair(0)
            with dve.Fori(1, CHUNKS // 2 - 1) as it:
                chunk_pair(it)
            chunk_pair(CHUNKS // 2 - 1)
            add_expert(CHUNKS * E - 1, 1, E - 1)

        @block.gpsimd
        def _(pool):
            tt = nc.gpsimd.tensor_tensor

            def split_ctx(g, slot):
                s = att[CROSS]
                dst = V[:, GT * slot:GT * (slot + 1)]
                pool.wait_ge(s["c_hi"], g + 1)
                tt(dst[:, :, 1, 0:DV], ctx_raw[:, slot], dst[:, :, 0, 0:DV], ALU.subtract).then_inc(s["c_lo"], 1)

            def normalise(ph, n, t):
                s = att[ph]
                pool.wait_ge(s["row_sum"], SUM_LINKS[ph] * (n + 1))
                for b in range(2):
                    p = prob[:, t % 2, :, b, :]
                    tt(p, p, sm[:, t % 2, b, :].unsqueeze(2).to_broadcast([P, NPAIR, S]), ALU.mult
                       ).then_inc(s["probs"], 1)

            def rotate(g, slot, js):
                s = att[SELF]
                for j in js:
                    r = ROTS * g + j
                    pool.wait_ge(s["cross"], r + 1)
                    is_k = j < KPAIR
                    h = 2 * j if is_k else 2 * (j - KPAIR)
                    v = (k_pair if is_k else q_pair)(slot, h)[0:RD]
                    tt(v, v, by_batch(cos_t[:]), ALU.mult).then_inc(s["rot_cos"], 1)
                    pool.wait_ge(s["rot_cos"], r + 1)
                    tt(v, v, rot[:, j % 2].rearrange("p (b h c) -> p b h c", h=2, c=S), ALU.add).then_inc(s["rotated"], 1)
                    acc = flat((acc_k if is_k else acc_q)[:])
                    if j in (1, KPAIR + 1):
                        tt(acc, sq[:, 0], sq[:, 1], ALU.add).then_inc(s["sq_added"], 1)
                    elif j > KPAIR:
                        pool.wait_ge(s["sq_added"], ADDS * g + adds_before(j - 1))
                        tt(acc, acc, sq[:, j % 2], ALU.add).then_inc(s["sq_added"], 1)

            def step(ph, it, t):
                n, gs = it * STEPS + t, it * 2
                ahead = gs + (t // GT + 2 if t % 2 else t // GT + 1)
                slot = (t // GT + (2 if t % 2 else 1)) % 2
                there = is_there(ahead, GROUPS)
                if ph == CROSS:
                    if t % 2 == 0 and there:
                        split_ctx(ahead, slot)
                elif there:
                    rotate(ahead, slot, range(0, 1) if t % 2 else range(6, 7))
                if is_there(n + 1, TILES):
                    normalise(ph, n + 1, (t + 1) % STEPS)
                if ph == SELF and there:
                    rotate(ahead, slot, range(1, 6) if t % 2 else range(7, 10))

            def attention(ph):
                if ph == CROSS:
                    split_ctx(0, 0)
                else:
                    rotate(0, 0, range(0, 10))
                    rotate(1, 1, range(0, 6))
                normalise(ph, 0, 0)
                for t in range(STEPS):
                    step(ph, 0, t)
                with pool.Fori(1, PASSES - 1) as it:
                    for t in range(STEPS):
                        step(ph, it, t)
                for t in range(STEPS):
                    step(ph, PASSES - 1, t)

            attention(CROSS)
            pool.wait_ge(pr["hi_s"], 7)
            tt(W_o[:, :, 1, :], Wo_raw, W_o[:, :, 0, :], ALU.subtract).then_inc(pr["lo_wo"], 1)
            attention(SELF)
            pool.wait_ge(pr["hi_e"], 5)
            tt(W_d[:, 1], q_flat[1][:, 0:2048].rearrange("p (e c) -> p e c", e=E), W_d[:, 0], ALU.subtract
               ).then_inc(pr["lo_wd"], 1)
            pool.wait_ge(pr["lo_e"], 4)
            pool.wait_ge(pr["lo_wd"], 1)

            def begin_total(c, u, uses):
                pool.wait_ge(ex[f"x_in{u}"], 16 * uses)
                pool.wait_ge(ex[f"y_in{u}"], 16 * uses)
                need(pool, ex[f"st{u}"], 16 * (uses - 1))
                tt(total[:, u], xc[:, u], yc[:, u], ALU.add).then_inc(ex["init"], 1)

            def chunk_pair(it):
                for u in range(2):
                    c = it * 2 + u
                    for e in range(E):
                        i = c * E + e
                        pool.wait_ge(ex["a_hi"], i + 1)
                        tt(actT[:, e % 2, 1], act_f[:, e % 2], actT[:, e % 2, 0], ALU.subtract
                           ).then_inc(ex["a_lo"], 1)
                        if e == 4 and is_there(c + 1, CHUNKS):
                            begin_total(c + 1, 1 - u, it + 1 + (1 if u else 0))

            begin_total(0, 0, 1)
            chunk_pair(0)
            with pool.Fori(1, CHUNKS // 2 - 1) as it:
                chunk_pair(it)
            chunk_pair(CHUNKS // 2 - 1)


_INS = ['x', 'ctx_1024', 'mask_BxS2_bf1', 'L0_xattn_Wq', 'L0_xattn_Wk', 'L0_xattn_Wv', 'L0_xattn_Wo',
        'L0_ffn_ln1_w', 'L0_ffn_ln2_w', 'L0_ffn_wq', 'L0_ffn_wk', 'L0_ffn_wv', 'L0_ffn_wo',
        'L0_ffn_qnorm_w', 'L0_ffn_knorm_w', 'L0_ffn_router_w', 'L0_ffn_router_bias', 'L0_ffn_wg',
        'L0_ffn_wu', 'L0_ffn_wd']
_ROWS = ('x', 'ctx_1024')


def shape_constants():
    import numpy as np

    f = np.float32
    inv_freq = (f(1.0) / f(1000000.0) ** (np.arange(0, RD, 2, dtype=f) / f(RD))).astype(f)
    ang = np.arange(S, dtype=f)[None, :] * inv_freq[:, None]
    cos = np.tile(np.cos(ang).astype(f), (2, GTOK // S))
    sin = np.tile(np.sin(ang).astype(f), (1, GTOK // S))
    rope = np.stack([cos, np.concatenate([sin, -sin])])
    causal = np.where(np.tril(np.ones((S, S), bool)), f(0.0), f(MASKED)).astype(f)
    earlier = np.tril(np.ones((E, E), f), -1).reshape(1, E * E)
    return {"eye": np.eye(P, dtype=f), "rope": rope.astype(f), "causal": causal, "earlier": earlier}


def kernel(**inputs):
    import numpy as _np
    import concourse.bacc as _bacc
    from concourse import mybir as _mybir
    from concourse.bass_utils import run_bass_kernel_spmd as _run

    nc = _bacc.Bacc("TRN2", target_bir_lowering=False, num_devices=1)
    arrays, args = {}, []

    def give(name, a):
        arrays[f"in_{name}_dram"] = a
        args.append(nc.dram_tensor(f"in_{name}_dram", a.shape, _mybir.dt.from_np(a.dtype), kind="ExternalInput").ap())

    for name in _INS:
        a = _np.ascontiguousarray(inputs[name])
        if a.dtype == bool:
            a = a.view(_np.uint8)
        if name in _ROWS:
            a = a.reshape(-1, a.shape[-1])
        give(name, a)
    for name, a in shape_constants().items():
        give(name, a)
    out = nc.dram_tensor("out_dram", (B * S, D), F32, kind="ExternalOutput").ap()
    build(nc, *args, out)
    r = _run(nc, [arrays], core_ids=[0])
    return r.results[0]["out_dram"].reshape(B, S, D)
```

```python
from contextlib import ExitStack

import concourse.bass as bass
from concourse import mybir

ALU = mybir.AluOpType
ACT = mybir.ActivationFunctionType
F32 = mybir.dt.float32
F32R = mybir.dt.float32r
BF16 = mybir.dt.bfloat16
I32 = mybir.dt.int32
U8 = mybir.dt.uint8
AX_X = mybir.AxisListType.X

P = 128
B, S, D = 64, 64, 256
DV = 128
H, HD = 16, 128
KVX, KVS = 8, 4
E, FI = 8, 128
TOPK = 2
RD = 64
HALF = RD // 2
KD = D // P
TILES = B * S // P
GT = 2
GROUPS = TILES // GT
GTOK = GT * P
STEPS = 4
PASSES = TILES // STEPS
NPAIR = H // 2
KPAIR = KVS // 2
K_BLOCKS = 2 + 2 * 4 * 2 * 2
SCORE_SCALE = 1.0 / float(HD) ** 0.5
MASKED = -1e30
LN_EPS = 1e-5
RMS_EPS = 1e-6
RSQRT_SEED = float(0x5F3759DF)
NEWTON = 3
RSQRT_LINKS = 2 + 3 * NEWTON

N_NORM_W = 2 * KD + H + KVS

CT = 4
CHUNKS = TILES // CT
CTOK = CT * P

CROSS, SELF = 0, 1
NORM_LINKS = {CROSS: 3 + RSQRT_LINKS, SELF: 1}
CHUNK_NORM_LINKS = 3 + RSQRT_LINKS
SCALE_LINKS = 3 + RSQRT_LINKS
TAIL_LINKS = {CROSS: 5 + RSQRT_LINKS, SELF: 2}
SUM_LINKS = {CROSS: 3, SELF: 2}
PROJ = {CROSS: NPAIR, SELF: KPAIR + NPAIR + GT}
ROTS = KPAIR + NPAIR
POOL_PAIRS = (0, KPAIR + 4)
TURNS = ROTS - len(POOL_PAIRS)
ROUTE_LINKS = 12


def need(eng, sem, value):
    if type(value) is int and value <= 0:
        return
    eng.wait_ge(sem, value)


def is_there(index, count):
    return type(index) is not int or index < count


class Chain:

    def __init__(self, eng, sem, run, links):
        self.eng, self.sem, self.run, self.links, self.k = eng, sem, run, links, 0

    def link(self, ins):
        self.k += 1
        ins.then_inc(self.sem, 1)
        self.eng.wait_ge(self.sem, self.run * self.links + self.k)

    def last(self, ins):
        self.k += 1
        ins.then_inc(self.sem, 1)
        assert self.k == self.links, (self.k, self.links)


def turn_of(j):
    return j - sum(p < j for p in POOL_PAIRS)


def flat(ap):
    return ap.rearrange("p h c -> p (h c)")


def build(nc, x, ctx_in, mask, Wq, Wk, Wv, Wo, ln1_w, ln2_w, wq, wk, wv, wo, qnorm_w, knorm_w,
          router_w, router_bias, wg, wu, wd, eye, rope, causal, earlier, out):
    x1_dram = nc.dram_tensor("x1_scratch", [B * S, D], F32, kind="Internal").ap()
    y_dram = nc.dram_tensor("y_scratch", [B * S, D], F32, kind="Internal").ap()
    y1_dram = nc.dram_tensor("y1_scratch", [B * S, D], F32, kind="Internal").ap()

    with ExitStack() as stack:
        def sb(name, shape, dt=F32):
            return stack.enter_context(nc.sbuf_tensor(name, shape, dt))

        def psum(name):
            return stack.enter_context(nc.psum_tensor(name, [P, 512], F32))

        def sem(name):
            return stack.enter_context(nc.semaphore(name))

        def sems(tag, names):
            return {name: sem(f"{name}_{tag}") for name in names}

        W = sb("weights", [P, 20480], F32R)
        hT = sb("hT", [P, 2, KD, GTOK], F32R)
        PT = sb("PT", [P, 2, NPAIR * P], F32R)
        U = sb("U", [P, 2, 2, NPAIR, P], F32R)
        V = sb("V", [P, STEPS, 2, KVS * HD], F32R)
        W_q = W[:, 0:8192].rearrange("p (l k c) -> p l k c", l=2, k=KD)
        W_o = W[:, 8192:16384].rearrange("p (h l c) -> p h l c", h=H, l=2)
        W_k = W[:, 16384:18432].rearrange("p (l k c) -> p l k c", l=2, k=KD)
        W_v = W[:, 18432:20480].rearrange("p (l k c) -> p l k c", l=2, k=KD)
        W_g = W[:, 0:4096].rearrange("p (l k c) -> p l k c", l=2, k=KD)
        W_u = W[:, 4096:8192].rearrange("p (l k c) -> p l k c", l=2, k=KD)
        W_d = W[:, 8192:12288].rearrange("p (l e c) -> p l e c", l=2, e=E)
        h2T = W[:, 12288:16384].rearrange("p (u l k c) -> p u l k c", u=2, l=2, k=KD)
        actT = W[:, 16384:18432].rearrange("p (u l c) -> p u l c", u=2, l=2)

        qT = sb("qT", [P, 2, 2 * GT, H, S])
        k_blocks = sb("k_blocks", [P, K_BLOCKS, S])
        kT = k_blocks[:, 1:K_BLOCKS - 1].rearrange("p (u h b) c -> p u h (b c)", u=2, h=4)
        prob = sb("prob", [P, 2, NPAIR, 2, S])
        xin = sb("xin", [P, 2, GT, D])
        xn = sb("xn", [P, GT, D])
        res = sb("res", [P, 2, GT, D])
        half_sum = sb("half_sum", [P, D])
        summed = sb("summed", [P, 2, D])
        ln_out = sb("ln_out", [P, 2, D])
        gram = sb("gram", [P, 2, KD, D], F32R)
        mask_rot = sb("mask_rot", [P, 2, 512])
        mask_all = mask_rot[:].rearrange("p a c -> p (a c)").bitcast(U8)
        swapped = mask_rot[RD:2 * RD]
        rot = mask_rot[0:RD]
        k_sq = sb("k_sq", [P, KPAIR, 512])
        ctx_raw = k_sq[:, 0].rearrange("p (u t c) -> p u t c", u=2, t=GT)
        wqT_stage = (k_sq[:, 1], flat(xn[:]))
        diag = sb("diag", [P, GT, P])
        any_valid = sb("any_valid", [P, B])
        mask_row = sb("mask_row", [1, 2, P], BF16)
        eye_f = sb("eye_f", [P, P])
        ones_f = sb("ones_f", [P, P])
        k_share = sb("k_share", [P, 1])
        ones_row = sb("ones_row", [1, P], BF16)
        causal_f = sb("causal_f", [S, S])
        causal_b = sb("causal_b", [S, S], BF16)
        eye2_b = sb("eye2_b", [S, 2, S], BF16)
        cos_t = sb("cos_t", [RD, GTOK])
        sin_all = sb("sin_all", [P, GTOK])
        sin_read = sin_all[0:RD]
        sin_t = sin_all[RD:2 * RD]
        norm_rows_w = sb("norm_rows_w", [N_NORM_W, P])
        norm_w = sb("norm_w", [P, N_NORM_W])
        ln_w = norm_w[:, 0:2 * KD].rearrange("p (n k) -> p n k", n=2)
        qk_w = norm_w[:, 2 * KD:]
        rt_raw = sb("rt_raw", [P, KD, E])
        rt_w = sb("rt_w", [P, KD, E])
        rt_bias = sb("rt_bias", [P, E])
        before = sb("before", [P, E, E])
        stat6 = sb("stat6", [P, CT, 6])
        stat = sb("stat", [P, CT, 2])
        tstat6 = sb("tstat6", [P, 6])
        tstat = sb("tstat", [P, 2])
        mx = sb("mx", [P, 2, 2, NPAIR])
        sm = sb("sm", [P, 2, 2, NPAIR])
        rs_v, rs_t, rs_y = sb("rs_v", [P, 4 * GT]), sb("rs_t", [P, 4 * GT]), sb("rs_y", [P, 4 * GT], I32)
        ts_v, ts_t, ts_y = sb("ts_v", [P, 1]), sb("ts_t", [P, 1]), sb("ts_y", [P, 1], I32)
        q_factor = sb("q_factor", [P, 2, 2 * GT])
        route = sb("route", [P, 5, CT, E])
        rank3 = k_sq[:, 1].rearrange("p (u t c) -> p u t c", u=2, t=CT)
        comb = sb("comb", [P, 2, CT, E])

        q_flat = [qT[:, i].rearrange("p b h c -> p (b h c)") for i in range(2)]
        Wo_raw = q_flat[1].rearrange("p (h c) -> p h c", h=H)
        fold_T = prob[:].rearrange("p u j b c -> p u (j b c)")
        yc = kT
        xc = fold_T.rearrange("p u (t d) -> p u t d", d=D)
        total = q_flat[0][:, 0:2048].rearrange("p (u t d) -> p u t d", u=2, t=CT)
        h_full = q_flat[0][:, 2048:4096].rearrange("p (u k c) -> p u k c", u=2, k=KD)
        th = q_flat[1][:, 0:1024].rearrange("p (u c) -> p u c", u=2)
        gated = q_flat[1][:, 1024:2048].rearrange("p (u c) -> p u c", u=2)
        act_f = q_flat[1][:, 2048:3072].rearrange("p (u c) -> p u c", u=2)
        yn = q_flat[1][:, 3072:4096].rearrange("p (t d) -> p t d", t=CT)

        b_score = [psum(f"b_score{i}") for i in range(2)]
        b_pv = [psum(f"b_pv{i}") for i in range(2)]
        b_proj = [psum(f"b_proj{i}") for i in range(2)]
        b_out = psum("b_out")
        b_misc = psum("b_misc")

        BOTH = ["x_in0", "x_in1", "r_in0", "r_in1", "sum_st0", "sum_st1", "norm_rows", "hT_ps", "hT_hi",
                "hT_lo", "proj_ps", "proj_ev", "score_ps", "row_max", "shifted", "expd", "row_sum", "probs",
                "pT_ps", "pT_hi", "pT_lo", "pv_ps", "u_hi", "u_lo", "out_ps", "tail"]
        att = [sems("x", BOTH + ["c_in0", "c_in1", "ln_st0", "ln_st1", "cT_ps", "cT", "c_hi", "c_lo", "mask_st"]),
               sems("s", BOTH + ["v_lo", "gram_ps", "gram_ev", "h_gram", "swap", "turned", "crossed", "rotated",
                                 "sq_added", "squares_ps", "scales", "factors", "rkb_ps", "k_scaled"])]
        eye_in, consts_in = sem("eye_in"), sem("consts_in")
        w_in = sems("in", ["Wk", "Wv", "Wq", "Wo", "wk", "wv", "wq", "wo", "wg", "wu", "wd"])
        pr = sems("prep", ["consts", "wkvT_ps", "wkvT", "wqT_ps", "wqT", "fold_ps", "fold_hi", "fold_lo",
                           "gramT_ps", "gramT", "gram_part", "gram_hi", "gram_lo", "hi_s", "lo_s", "lo_wo", "hi_e", "lo_e", "lo_wd", "rt_w", "normT_ps", "normT"])
        ex = sems("e", ["y_in0", "y_in1", "x_in0", "x_in1", "st0", "st1", "norm_rows", "scaled", "T_ps", "h_full",
                        "h_hi", "h_lo", "rt_ps", "rt_exp", "routed", "gate_ps", "up_ps", "tanh", "gated",
                        "act", "a_hi", "a_lo", "down_ps", "added", "init"])
        N_CONSTS = 11 * 16

        def rsqrt(ch, var, v, t, y, n, eps=None):
            if var is not None:
                ch.link(nc.vector.tensor_scalar(v[:, 0:n], var, eps, None, ALU.add))
            v, t, y = v[:, 0:n], t[:, 0:n], y[:, 0:n]
            yf = y.bitcast(F32)
            ch.link(nc.vector.tensor_scalar(y, v.bitcast(I32), -0.5, RSQRT_SEED, ALU.mult, ALU.add))
            for _ in range(NEWTON):
                ch.link(nc.vector.tensor_tensor(t, yf, yf, ALU.mult))
                ch.link(nc.vector.scalar_tensor_tensor(out=t, in0=t, scalar=-0.5, in1=v,
                                                       op0=ALU.mult, op1=ALU.mult))
                ch.link(nc.vector.scalar_tensor_tensor(out=yf, in0=t, scalar=1.5, in1=yf,
                                                       op0=ALU.add, op1=ALU.mult))
            return yf

        def q_pair(slot, h):
            return qT[:, slot, :, h:h + 2, :]

        def k_pair(slot, h):
            return kT[:, slot, h:h + 2, :].rearrange("p h (b c) -> p b h c", c=S)

        def by_batch(ap):
            return ap.rearrange("p (b c) -> p b c", c=S).unsqueeze(2).to_broadcast(
                [ap.shape[0], 2 * GT, 2, S])

        def proj_bank(ph, j):
            return b_proj[(j + (1 if ph == SELF else 0)) % 2]

        halves_of_heads = (slice(0, NPAIR), slice(NPAIR, H))

        def pairs_of(ap):
            return ap.rearrange("p (j c) -> p j c", j=NPAIR)

        block = stack.enter_context(nc.Block())

        @block.sync
        def _(sp):
            rows_in = [x, y_dram]

            def rows(dram, g):
                return dram[bass.ds(g * GTOK, GTOK), :].rearrange("(t p) c -> p t c", p=P)

            def load_rows(ph, g, slot):
                if is_there(g, GROUPS):
                    need(sp, att[ph]["norm_rows"], NORM_LINKS[ph] * (g - 1))
                    sp.dma_start(xin[:, slot], rows(rows_in[ph], g)).then_inc(att[ph][f"x_in{slot}"], 16)

            def load_ctx(g, slot):
                if is_there(g, GROUPS):
                    need(sp, att[CROSS]["cT_ps"], g - 1)
                    need(sp, att[CROSS]["c_lo"], g - 1)
                    sp.dma_start(ctx_raw[:, slot], rows(ctx_in, g)).then_inc(att[CROSS][f"c_in{slot}"], 16)

            def load_res(ph, g, slot):
                if is_there(g, GROUPS):
                    need(sp, att[ph]["tail"], TAIL_LINKS[ph] * GT * (g - 1))
                    sp.dma_start(res[:, slot], rows(rows_in[ph], g)).then_inc(att[ph][f"r_in{slot}"], 16)

            def store(ph, n, slot):
                s = att[ph]
                sp.wait_ge(s["tail"], TAIL_LINKS[ph] * (n + 1))
                if ph == CROSS:
                    sp.dma_start(x1_dram[bass.ds(n * P, P), :], summed[:, slot]).then_inc(s[f"sum_st{slot}"], 16)
                    sp.dma_start(y_dram[bass.ds(n * P, P), :], ln_out[:, slot]).then_inc(s[f"ln_st{slot}"], 16)
                else:
                    sp.dma_start(y1_dram[bass.ds(n * P, P), :], summed[:, slot]).then_inc(s[f"sum_st{slot}"], 16)

            def weights(dst, src, name):
                sp.dma_start(dst.rearrange("p (k c) -> p k c", k=KD),
                             src.rearrange("(k p) c -> p k c", p=P)).then_inc(w_in[name], 16)

            def next_weights(ph, slot):
                sp.wait_ge(att[ph]["score_ps"], 2 * (TILES - (GT if slot == 0 else 0)))
                if ph == CROSS and slot == 0:
                    weights(flat(kT[:, 0])[:, 0:1024], wk, "wk")
                    weights(q_flat[0], wq, "wq")
                elif ph == CROSS:
                    weights(flat(kT[:, 1])[:, 0:1024], wv, "wv")
                    sp.dma_start(Wo_raw, wo.rearrange("(h p) c -> p h c", p=P)).then_inc(w_in["wo"], 16)
                elif slot == 0:
                    for k in range(KD):
                        for dst, src, name in ((q_flat[0][:, 0:2048], wg, "wg"), (q_flat[0][:, 2048:4096], wu, "wu")):
                            sp.dma_start(dst.rearrange("p (k e i) -> p k e i", k=KD, e=E)[:, k],
                                         src[:, k * P:(k + 1) * P, :].rearrange("e p i -> p e i")
                                         ).then_inc(w_in[name], 16)
                else:
                    sp.dma_start(q_flat[1][:, 0:2048].rearrange("p (e c) -> p e c", e=E),
                                 wd.rearrange("e p c -> p e c")).then_inc(w_in["wd"], 16)

            def attention_pass(ph, it, last=False):
                for t in range(STEPS):
                    n, g = it * STEPS + t, it * 2 + t // GT
                    if last and t >= GT:
                        next_weights(ph, t - GT)
                    if t % GT == 0:
                        load_rows(ph, g + 2, t // GT)
                        if ph == CROSS:
                            load_ctx(g + 2, t // GT)
                        load_res(ph, g + 1, (t // GT + 1) % 2)
                    if type(n) is not int or n > 0:
                        store(ph, n - 1, (t - 1) % 2)

            def all_passes(ph):
                attention_pass(ph, 0)
                with sp.Fori(1, PASSES - 1) as it:
                    attention_pass(ph, it)
                attention_pass(ph, PASSES - 1, last=True)
                store(ph, TILES - 1, (TILES - 1) % 2)

            sp.dma_start(eye_f[:], eye).then_inc(eye_in, 16)
            sp.dma_start(flat(kT[:, 0]), Wk).then_inc(w_in["Wk"], 16)
            sp.dma_start(flat(kT[:, 1]), Wv).then_inc(w_in["Wv"], 16)
            weights(q_flat[0], Wq, "Wq")
            sp.dma_start(Wo_raw, Wo.rearrange("(h p) c -> p h c", p=P)).then_inc(w_in["Wo"], 16)
            load_rows(CROSS, 0, 0)
            load_rows(CROSS, 1, 1)
            load_ctx(0, 0)
            load_ctx(1, 1)
            load_res(CROSS, 0, 0)
            sp.dma_start(mask_all, mask.rearrange("(a b) s -> a (b s)", a=1)
                         .to_broadcast([P, B * S])).then_inc(consts_in, 16)
            for dst, src in ((causal_f[:], causal), (cos_t[:], rope[0]), (sin_all[:], rope[1:3].rearrange("a p c -> (a p) c")),
                             (norm_rows_w[0:KD], ln1_w.rearrange("(k p) -> k p", p=P)),
                             (norm_rows_w[KD:2 * KD], ln2_w.rearrange("(k p) -> k p", p=P)),
                             (norm_rows_w[2 * KD:2 * KD + H], qnorm_w.rearrange("(h p) -> h p", p=P)),
                             (norm_rows_w[2 * KD + H:], knorm_w.rearrange("(h p) -> h p", p=P)),
                             (rt_raw[:], router_w.rearrange("(k p) e -> p k e", p=P)),
                             (rt_bias[:], router_bias.rearrange("(a e) -> a e", a=1).to_broadcast([P, E])),
                             (before[:].rearrange("p a b -> p (a b)"), earlier.to_broadcast([P, E * E]))):
                sp.dma_start(dst, src).then_inc(consts_in, 16)
            all_passes(CROSS)

            for slot in range(2):
                sp.wait_ge(att[CROSS][f"sum_st{slot}"], 16 * TILES // 2)
                sp.wait_ge(att[CROSS][f"ln_st{slot}"], 16 * TILES // 2)
            load_rows(SELF, 0, 0)
            load_rows(SELF, 1, 1)
            load_res(SELF, 0, 0)
            all_passes(SELF)

            for slot in range(2):
                sp.wait_ge(att[SELF][f"sum_st{slot}"], 16 * TILES // 2)
            sp.wait_ge(att[SELF]["pT_ps"], 2 * TILES)

            def chunk_rows(dram, c):
                return dram[bass.ds(c * CTOK, CTOK), :].rearrange("(t p) d -> p t d", p=P)

            def load_chunk(c, slot):
                if is_there(c, CHUNKS):
                    need(sp, ex["scaled"], c - 1)
                    need(sp, ex["init"], c - 1)
                    sp.dma_start(yc[:, slot], chunk_rows(y1_dram, c)).then_inc(ex[f"y_in{slot}"], 16)
                    sp.dma_start(xc[:, slot], chunk_rows(x1_dram, c)).then_inc(ex[f"x_in{slot}"], 16)

            def chunk_pair(it):
                for u in range(2):
                    c = it * 2 + u
                    load_chunk(c + 2, u)
                    sp.wait_ge(ex["added"], E * CT * (c + 1))
                    sp.dma_start(chunk_rows(out, c), total[:, u]).then_inc(ex[f"st{u}"], 16)

            load_chunk(0, 0)
            load_chunk(1, 1)
            chunk_pair(0)
            with sp.Fori(1, CHUNKS // 2 - 1) as it:
                chunk_pair(it)
            chunk_pair(CHUNKS // 2 - 1)
            for u in range(2):
                sp.wait_ge(ex[f"st{u}"], 16 * CHUNKS // 2)

        @block.tensor
        def _(pe):
            def mm(dst, lhsT, rhs, start, stop=True):
                return nc.tensor.matmul(dst, lhsT, rhs, start=start, stop=stop, skip_group_check=True)

            def mm3(dst, st, mv, first, final):
                mm(dst, st(0), mv(0), start=first, stop=False)
                mm(dst, st(0), mv(1), start=False, stop=False)
                return mm(dst, st(1), mv(0), start=False, stop=final)

            def transpose_q(j, name):
                if j < NPAIR:
                    need(pe, pr[name], j - 1)
                    for i in range(2):
                        for k in range(KD):
                            c = (2 * j + i) * HD
                            last = nc.tensor.transpose(
                                b_proj[j % 2][:, (2 * i + k) * P:(2 * i + k + 1) * P],
                                q_flat[0].rearrange("p (k c) -> p k c", k=KD)[:, k, c:c + HD], eye_f[:])
                    last.then_inc(pr[name + "_ps"], 1)

            def gram_weights():
                pe.wait_ge(w_in["wq"], 16)
                pe.wait_ge(att[CROSS]["shifted"], 2 * TILES)
                transpose_q(0, "gramT")
                for j in range(NPAIR):
                    transpose_q(j + 1, "gramT")
                    pe.wait_ge(pr["gramT"], j + 1)
                    for i in range(2):
                        for m in range(KD):
                            last = mm(b_score[m][:, 0:D], mask_rot[:, j % 2, (2 * i + m) * P:(2 * i + m + 1) * P],
                                      mask_rot[:, j % 2, 2 * i * P:2 * i * P + D],
                                      start=j == 0 and i == 0, stop=j == NPAIR - 1 and i == 1)
                    last.then_inc(pr["gram_part"], 1)

            def fold_weights():
                pe.wait_ge(eye_in, 16)
                for i, (name, dst) in enumerate((("Wk", b_score), ("Wv", b_pv))):
                    pe.wait_ge(w_in[name], 16)
                    for j in range(KVX):
                        last = nc.tensor.transpose(dst[j // 4][:, j % 4 * P:(j % 4 + 1) * P],
                                                   flat(kT[:, i])[:, j * P:(j + 1) * P], eye_f[:])
                        if j % 4 == 3:
                            last.then_inc(pr["wkvT_ps"], 1)

                pe.wait_ge(w_in["Wq"], 16)
                transpose_q(0, "wqT")
                pe.wait_ge(pr["wkvT"], 4)
                pe.wait_ge(w_in["Wo"], 16)
                for j in range(NPAIR):
                    transpose_q(j + 1, "wqT")
                    pe.wait_ge(pr["wqT"], j + 1)
                    need(pe, pr["fold_hi"], 2 * j - 3)
                    need(pe, pr["fold_lo"], 2 * j - 3)
                    dst = (b_out, b_misc)[j % 2]
                    for i in range(2):
                        for k in range(KD):
                            c = (2 * i + k) * P
                            last = mm(dst[:, c:c + P], wqT_stage[j % 2][:, c:c + P],
                                      fold_T[:, 0, j * P:(j + 1) * P], start=True)
                    last.then_inc(pr["fold_ps"], 1)
                    need(pe, pr["fold_hi"], 2 * j - 2)
                    need(pe, pr["fold_lo"], 2 * j - 2)
                    for i in range(2):
                        last = mm(b_score[j % 2][:, i * D:(i + 1) * D],
                                  fold_T[:, 1, j * P:(j + 1) * P], Wo_raw[:, 2 * j + i, :], start=True)
                    last.then_inc(pr["fold_ps"], 1)

            def transpose_rows(ph, g):
                s = att[ph]
                pe.wait_ge(s["norm_rows"], NORM_LINKS[ph] * (g + 1))
                need(pe, *((s["cT"], g) if ph == CROSS else (s["k_scaled"], g)))
                for k in range(KD):
                    for i in range(GT):
                        c = k * GTOK + i * P
                        last = nc.tensor.transpose(b_misc[:, c:c + P], xn[:, i, k * P:(k + 1) * P], eye_f[:])
                last.then_inc(s["hT_ps"], 1)

            def transpose_ctx(g, slot):
                s = att[CROSS]
                pe.wait_ge(s[f"c_in{slot}"], 16 * (g // 2 + 1) if type(g) is int else g_uses(g, slot))
                pe.wait_ge(s["hT_hi"], g + 1)
                pe.wait_ge(s["hT_lo"], g + 1)
                for i in range(GT):
                    last = nc.tensor.transpose(b_misc[:, i * P:(i + 1) * P], ctx_raw[:, slot, i, :], eye_f[:])
                last.then_inc(s["cT_ps"], 1)

            def bank_free(ph, g, j):
                s = att[ph]
                if ph == SELF and j == 1:
                    pe.wait_ge(s["gram_ev"], g + 1)
                else:
                    need(pe, s["proj_ev"], PROJ[ph] * g + j - 1)
                if ph == SELF and j == 0:
                    need(pe, s["v_lo"], GT * g - 1)

            def project_gram(g):
                s = att[SELF]
                need(pe, s["proj_ev"], PROJ[SELF] * g)
                need(pe, s["v_lo"], GT * g)
                for m in range(KD):
                    for k in range(KD):
                        last = mm3(b_proj[0][:, m * GTOK:(m + 1) * GTOK],
                                   lambda l: gram[:, l, k, m * P:(m + 1) * P],
                                   lambda l: hT[:, l, k, :], first=k == 0, final=k == KD - 1)
                last.then_inc(s["gram_ps"], 1)

            def project_pair(ph, g, j, w, col):
                bank_free(ph, g, j)
                for i in range(2):
                    for k in range(KD):
                        last = mm3(proj_bank(ph, j)[:, i * GTOK:(i + 1) * GTOK],
                                   lambda l: w[:, l, k, col + i * HD:col + (i + 1) * HD],
                                   lambda l: hT[:, l, k, :], first=k == 0, final=k == KD - 1)
                last.then_inc(att[ph]["proj_ps"], 1)

            def project_v(g, j, i):
                bank_free(SELF, g, j)
                for k in range(KD):
                    last = mm3(proj_bank(SELF, j)[:], lambda l: hT[:, l, k, i * P:(i + 1) * P],
                               lambda l: W_v[:, l, k, :], first=k == 0, final=k == KD - 1)
                last.then_inc(att[SELF]["proj_ps"], 1)

            def first_work(ph, g):
                s = att[ph]
                pe.wait_ge(s["hT_hi"], g + 1)
                pe.wait_ge(s["hT_lo"], g + 1)
                if ph == CROSS:
                    for j in range(4):
                        project_pair(ph, g, j, W_q, 2 * j * HD)
                else:
                    project_gram(g)
                    for j in range(KPAIR):
                        project_pair(ph, g, j, W_k, 2 * j * HD)
                    for j in range(4):
                        project_pair(ph, g, KPAIR + j, W_q, 2 * j * HD)

            def second_work(ph, g):
                s = att[ph]
                if ph == CROSS:
                    for j in range(4, 8):
                        project_pair(ph, g, j, W_q, 2 * j * HD)
                    return
                for j in range(4, 8):
                    project_pair(ph, g, KPAIR + j, W_q, 2 * j * HD)
                pe.wait_ge(s["factors"], g + 1)
                for i in range(GT):
                    last = mm(b_misc[:, GTOK + i * P:GTOK + (i + 1) * P], ones_f[:], diag[:, i, :], start=True)
                last.then_inc(s["rkb_ps"], 1)
                for i in range(GT):
                    project_v(g, KPAIR + NPAIR + i, i)

            def square_sums(g):
                s = att[SELF]
                pe.wait_ge(s["sq_added"], 2 * (g + 1))
                pe.wait_ge(s["h_gram"], g + 1)
                for i in range(GT):
                    for a in range(2):
                        c = a * GTOK + i * P
                        mm(b_misc[:, i:i + 1], k_sq[:, 0, c:c + P], k_share[:], start=a == 0, stop=a == 1)
                for i in range(2 * GT):
                    last = mm(b_misc[:, GT + i:GT + i + 1], k_sq[:, 1, i * P:(i + 1) * P], ones_f[:, 0:1], start=True)
                last.then_inc(s["squares_ps"], 1)

            def scores(ph, n, g, t):
                s = att[ph]
                if ph == CROSS:
                    pe.wait_ge(s["proj_ev"], PROJ[ph] * (g + 1))
                    pe.wait_ge(s["cT"], g + 1)
                    pe.wait_ge(s["mask_st"], n + 1)
                else:
                    pe.wait_ge(s["rotated"], ROTS * (g + 1))
                    pe.wait_ge(s["k_scaled"], g + 1)
                slot, base = t // GT % 2, t % GT * P
                for b in range(2):
                    need(pe, s["shifted"], 2 * n + b - 1)
                    dst, tok = b_score[b], base + b * S
                    if ph == CROSS:
                        mm(pairs_of(dst[:]), ones_row[:], mask_row[0:1, t % 2, b * S:(b + 1) * S]
                           .unsqueeze(1).to_broadcast([1, NPAIR, S]), start=True, stop=False)
                    else:
                        mm(pairs_of(dst[:]), eye2_b[:].rearrange("p a c -> p (a c)"),
                           causal_b[:].unsqueeze(1).to_broadcast([S, NPAIR, S]), start=True, stop=False)
                    for j in range(NPAIR):
                        kv = 0 if ph == CROSS else j // 2
                        own = 1 + (slot * 4 + kv) * 2 * GT + tok // S
                        if j < NPAIR - 1:
                            cols, key = j, k_blocks[:, own:K_BLOCKS:K_BLOCKS - 1 - own]
                        else:
                            cols, key = j - 1, k_blocks[:, 0:own + 1:own]
                        last = mm(dst[:, cols * S:(cols + 2) * S].rearrange("p (a c) -> p a c", a=2),
                                  qT[:, slot, tok // S, 2 * j:2 * j + 2, :].rearrange("p h c -> p (h c)"), key,
                                  start=False)
                    last.then_inc(s["score_ps"], 1)

            def transpose_probs(ph, n, t):
                s = att[ph]
                pe.wait_ge(s["probs"], 2 * n + 2)
                need(pe, s["u_hi"], 4 * n)
                need(pe, s["u_lo"], 4 * n)
                for j in range(NPAIR):
                    last = nc.tensor.transpose(b_pv[j // 4][:, j % 4 * P:(j % 4 + 1) * P],
                                               prob[:, t % 2, j].rearrange("p b c -> p (b c)"), eye_f[:])
                    if j % 4 == 3:
                        last.then_inc(s["pT_ps"], 1)

            def prob_v(ph, n, t, half):
                s = att[ph]
                if half == 0:
                    pe.wait_ge(s["pT_hi"], 2 * n + 2)
                    pe.wait_ge(s["pT_lo"], 2 * n + 2)
                    if ph == CROSS:
                        pe.wait_ge(s["c_lo"], n_group(n, t) + 1)
                    else:
                        pe.wait_ge(s["v_lo"], n + 1)
                        pe.wait_ge(s["proj_ev"], PROJ[ph] * (n_group(n, t) + 1) - (GT - 1 - t % GT))
                for b in range(2):
                    if half == 1:
                        pe.wait_ge(s["u_hi"], 4 * n + b + 1)
                        pe.wait_ge(s["u_lo"], 4 * n + b + 1)
                    rows = slice(b * S, (b + 1) * S)
                    if ph == CROSS:
                        last = mm3(b_pv[b][:], lambda l: V[rows, t, l, 0:DV],
                                   lambda l: PT[rows, l, half * 512:(half + 1) * 512], first=True, final=True)
                    else:
                        for a in range(2):
                            c, kv = half * 512 + a * 256, half * 2 + a
                            last = mm3(b_pv[b][:, a * 256:(a + 1) * 256],
                                       lambda l: V[rows, t, l, kv * HD:(kv + 1) * HD],
                                       lambda l: PT[rows, l, c:c + 256], first=True, final=True)
                    last.then_inc(s["pv_ps"], 1)

            def n_group(n, t):
                return n // GT if type(n) is int else group_of[t]

            def project_out(ph, n, half):
                s = att[ph]
                pe.wait_ge(s["u_hi"], 4 * n + 2 * half + 2)
                pe.wait_ge(s["u_lo"], 4 * n + 2 * half + 2)
                if half == 0:
                    need(pe, s["tail"], TAIL_LINKS[ph] * (n - 1) + 2 if type(n) is not int or n > 0 else 0)
                for i in range(NPAIR):
                    h = half * NPAIR + i
                    mm(b_out[:], U[:, half, 0, i, :], W_o[:, h].rearrange("p l c -> p (l c)"),
                       start=h == 0, stop=False)
                    last = mm(b_out[:, 0:D], U[:, half, 1, i, :], W_o[:, h, 0, :], start=False, stop=h == H - 1)
                if half == 1:
                    last.then_inc(s["out_ps"], 1)

            group_of = {}
            uses_of = {}

            def g_uses(g, slot):
                return uses_of[slot]

            def step(ph, it, t):
                n = it * STEPS + t
                gs = it * 2
                group_of[t] = gs + t // GT
                transpose_probs(ph, n, t)
                ahead = gs + (t // GT + 2 if t % 2 else t // GT + 1)
                if t % 2:
                    if is_there(ahead, GROUPS):
                        transpose_rows(ph, ahead)
                elif ph == CROSS and is_there(ahead, GROUPS):
                    slot = (t // GT + 1) % 2
                    uses_of[slot] = (it + (t // GT + 1) // 2) * 16 + 16
                    transpose_ctx(ahead, slot)
                if is_there(n + 1, TILES):
                    scores(ph, n + 1, gs + (t + 1) // GT, (t + 1) % STEPS)
                if is_there(ahead, GROUPS):
                    (first_work if t % 2 else second_work)(ph, ahead)
                prob_v(ph, n, t, 0)
                if type(n) is not int or n > 0:
                    project_out(ph, n - 1, 1)
                prob_v(ph, n, t, 1)
                project_out(ph, n, 0)
                if ph == SELF and t % 2 and is_there(ahead, GROUPS):
                    square_sums(ahead)

            def attention(ph):
                transpose_rows(ph, 0)
                if ph == CROSS:
                    transpose_ctx(0, 0)
                first_work(ph, 0)
                if ph == SELF:
                    square_sums(0)
                second_work(ph, 0)
                if ph == SELF:
                    pe.wait_ge(pr["hi_s"], 8)
                    pe.wait_ge(pr["lo_wo"], 2)
                transpose_rows(ph, 1)
                first_work(ph, 1)
                if ph == SELF:
                    square_sums(1)
                scores(ph, 0, 0, 0)
                for t in range(STEPS):
                    step(ph, 0, t)
                with pe.Fori(1, PASSES - 1) as it:
                    for t in range(STEPS):
                        step(ph, it, t)
                for t in range(STEPS):
                    step(ph, PASSES - 1, t)
                project_out(ph, TILES - 1, 1)

            fold_weights()
            pe.wait_ge(consts_in, N_CONSTS)
            nc.tensor.transpose(b_proj[0][:, 0:N_NORM_W], norm_rows_w[:], eye_f[0:N_NORM_W, 0:N_NORM_W]
                                ).then_inc(pr["normT_ps"], 1)
            pe.wait_ge(pr["normT"], 1)
            pe.wait_ge(pr["fold_hi"], 2 * NPAIR)
            pe.wait_ge(pr["fold_lo"], 2 * NPAIR)
            pe.wait_ge(pr["consts"], 1)
            attention(CROSS)
            gram_weights()
            pe.wait_ge(pr["gram_hi"], KD)
            pe.wait_ge(pr["gram_lo"], KD)
            pe.wait_ge(pr["hi_s"], 6)
            pe.wait_ge(pr["lo_s"], 6)
            attention(SELF)

            pe.wait_ge(pr["rt_w"], 1)
            t_banks = (b_out, b_misc)

            def transpose_chunk(c):
                pe.wait_ge(ex["scaled"], c + 1)
                need(pe, ex["rt_exp"], c)
                need(pe, ex["h_lo"], c)
                for k in range(KD):
                    for i in range(CT):
                        last = nc.tensor.transpose(t_banks[k][:, i * P:(i + 1) * P],
                                                   yn[:, i, k * P:(k + 1) * P], eye_f[:])
                last.then_inc(ex["T_ps"], 1)

            def router(c, u):
                pe.wait_ge(ex["h_full"], c + 1)
                pe.wait_ge(ex["h_hi"], c + 1)
                pe.wait_ge(ex["h_lo"], c + 1)
                for i in range(CT):
                    for k in range(KD):
                        last = mm(b_out[:, i * E:(i + 1) * E], h_full[:, u, k, i * P:(i + 1) * P],
                                  rt_w[:, k, :], start=k == 0, stop=k == KD - 1)
                last.then_inc(ex["rt_ps"], 1)

            def gate_up(c, u, e):
                i = c * E + e
                pe.wait_ge(ex["h_hi"], c + 1)
                pe.wait_ge(ex["h_lo"], c + 1)
                need(pe, ex["gated"], i - 1)
                for k in range(KD):
                    last = mm3(b_score[e % 2][:], lambda l: W_g[:, l, k, e * FI:(e + 1) * FI],
                               lambda l: h2T[:, u, l, k, :], first=k == 0, final=k == KD - 1)
                last.then_inc(ex["gate_ps"], 1)
                need(pe, ex["act"], i - 1)
                for k in range(KD):
                    last = mm3(b_pv[e % 2][:], lambda l: W_u[:, l, k, e * FI:(e + 1) * FI],
                               lambda l: h2T[:, u, l, k, :], first=k == 0, final=k == KD - 1)
                last.then_inc(ex["up_ps"], 1)

            def down(i, e):
                pe.wait_ge(ex["a_hi"], i + 1)
                pe.wait_ge(ex["a_lo"], i + 1)
                for b in range(2):
                    need(pe, ex["added"], CT * i - 2 + 2 * b if type(i) is not int or i > 0 else 0)
                    for a in range(2):
                        c = (2 * b + a) * P
                        last = mm3(b_proj[b][:, a * D:(a + 1) * D], lambda l: actT[:, e % 2, l, c:c + P],
                                   lambda l: W_d[:, l, e, :], first=True, final=True)
                    last.then_inc(ex["down_ps"], 1)

            def chunk_pair(it):
                for u in range(2):
                    c = it * 2 + u
                    for e in range(E):
                        gate_up(c, u, e)
                        i = c * E + e
                        if type(i) is not int or i > 0:
                            down(i - 1, (e - 1) % E)
                        if e == 3 and is_there(c + 1, CHUNKS):
                            transpose_chunk(c + 1)
                        if e == 5 and is_there(c + 1, CHUNKS):
                            router(c + 1, 1 - u)

            transpose_chunk(0)
            router(0, 0)
            pe.wait_ge(pr["hi_e"], 5)
            pe.wait_ge(pr["lo_e"], 4)
            pe.wait_ge(pr["lo_wd"], 1)
            chunk_pair(0)
            with pe.Fori(1, CHUNKS // 2 - 1) as it:
                chunk_pair(it)
            chunk_pair(CHUNKS // 2 - 1)
            down(CHUNKS * E - 1, E - 1)

        @block.scalar
        def _(act):
            def copy(dst, src, scale=1.0):
                return nc.scalar.activation(dst, src, ACT.Copy, scale=scale)

            def fold_weights():
                for i in range(4):
                    act.wait_ge(pr["wkvT_ps"], i + 1)
                    copy(fold_T[:, i // 2, i % 2 * 512:(i % 2 + 1) * 512], (b_score, b_pv)[i // 2][i % 2][:]).then_inc(pr["wkvT"], 1)

                def split_high(j):
                    act.wait_ge(pr["fold_ps"], 2 * j + 1)
                    copy(W_q[:, 0, :, 2 * j * HD:2 * (j + 1) * HD].rearrange("p k (h c) -> p h k c", h=2),
                         (b_out, b_misc)[j % 2][:].rearrange("p (h k c) -> p h k c", h=2, k=KD)
                         ).then_inc(pr["fold_hi"], 1)
                    act.wait_ge(pr["fold_ps"], 2 * j + 2)
                    copy(W_o[:, 2 * j:2 * j + 2, 0, :],
                         b_score[j % 2][:].rearrange("p (h c) -> p h c", h=2)).then_inc(pr["fold_hi"], 1)

                for j in range(NPAIR + 1):
                    if j < NPAIR:
                        act.wait_ge(pr["wqT_ps"], j + 1)
                        need(act, pr["fold_ps"], 2 * j - 3)
                        copy(wqT_stage[j % 2], b_proj[j % 2][:]).then_inc(pr["wqT"], 1)
                    if j > 0:
                        split_high(j - 1)
                act.wait_ge(pr["normT_ps"], 1)
                copy(norm_w[:], b_proj[0][:, 0:N_NORM_W]).then_inc(pr["normT"], 1)

            def rows_high(ph, g):
                s = att[ph]
                act.wait_ge(s["hT_ps"], g + 1)
                need(act, s["proj_ps"], PROJ[ph] * g)
                copy(hT[:, 0], b_misc[:].rearrange("p (k c) -> p k c", k=KD)).then_inc(s["hT_hi"], 1)

            def stage_mask(n, slot):
                s = att[CROSS]
                if is_there(n, TILES):
                    need(act, s["score_ps"], 2 * (n - 1))
                    nc.scalar.activation(mask_row[0:1, slot, :], mask_all[0:1, bass.ds(n * P, P)], ACT.Copy,
                                         scale=-MASKED, bias=MASKED).then_inc(s["mask_st"], 1)

            def ctx_copy(g, slot):
                s = att[CROSS]
                act.wait_ge(s["cT_ps"], g + 1)
                need(act, s["pv_ps"], 4 * GT * (g - 1))
                copy(V[:, GT * slot:GT * (slot + 1), 0, 0:DV], ctx_raw[:, slot]).then_inc(s["c_hi"], 1)
                act.wait_ge(s["cT_ps"], g + 1)
                copy(kT[:, slot, 0, :], b_misc[:, 0:GTOK]).then_inc(s["cT"], 1)

            def read_pair(ph, g, slot, j):
                s = att[ph]
                act.wait_ge(s["proj_ps"], PROJ[ph] * g + j + 1)
                src = proj_bank(ph, j)[:]
                if ph == CROSS:
                    for i in range(2):
                        last = copy(qT[:, slot, :, 2 * j + i, :],
                                    src[:, i * GTOK:(i + 1) * GTOK].rearrange("p (b c) -> p b c", c=S))
                    last.then_inc(s["proj_ev"], 1)
                    return
                is_k = j < KPAIR
                h = 2 * j if is_k else 2 * (j - KPAIR)
                for i in range(2):
                    dst = (k_pair if is_k else q_pair)(slot, h)[:, :, i, :]
                    col = (H if is_k else 0) + h + i
                    last = copy(dst, src[:, i * GTOK:(i + 1) * GTOK].rearrange("p (b c) -> p b c", c=S),
                                scale=qk_w[:, col:col + 1])
                if is_k:
                    need(act, s["squares_ps"], g)
                    last = nc.scalar.activation(k_sq[:, j], src, ACT.Square)
                last.then_inc(s["proj_ev"], 1)

            def swap_halves(g, slot, j):
                s = att[SELF]
                i = turn_of(j)
                act.wait_ge(s["proj_ev"], PROJ[SELF] * g + j + 1)
                need(act, s["turned"], TURNS * g + i - 1)
                h = 2 * j if j < KPAIR else 2 * (j - KPAIR)
                src = (k_pair if j < KPAIR else q_pair)(slot, h)
                for a, b in ((0, HALF), (HALF, 0)):
                    last = copy(swapped[a:a + HALF, i % 2].rearrange("p (b h c) -> p b h c", h=2, c=S),
                                src[b:b + HALF])
                last.then_inc(s["swap"], 1)

            def read_gram(g):
                s = att[SELF]
                act.wait_ge(s["gram_ps"], g + 1)
                for k in range(KD):
                    c = slice(k * GTOK, (k + 1) * GTOK)
                    last = copy(flat(xn[:])[:, c], b_proj[0][:, c], scale=ln_w[:, 0, k:k + 1])
                last.then_inc(s["gram_ev"], 1)

            def read_v(g, gslot, i):
                s = att[SELF]
                j = KPAIR + NPAIR + i
                act.wait_ge(s["proj_ps"], PROJ[SELF] * g + j + 1)
                copy(V[:, GT * gslot + i, 0, :], proj_bank(SELF, j)[:]).then_inc(s["proj_ev"], 1)

            def exps(ph, n, t, b):
                s = att[ph]
                act.wait_ge(s["shifted"], 2 * n + b + 1)
                scale = SCORE_SCALE
                if ph == SELF:
                    i = t % GT * 2 + b
                    if b == 0:
                        act.wait_ge(s["factors"], group_of[t] + 1)
                    scale = q_factor[:, t // GT, i:i + 1]
                p = prob[:, t % 2, :, b, :]
                nc.scalar.activation(p, p, ACT.Exp, scale=scale).then_inc(s["expd"], 1)

            def probs_high(ph, n):
                s = att[ph]
                for i in range(2):
                    act.wait_ge(s["pT_ps"], 2 * n + i + 1)
                    copy(PT[:, 0, i * 512:(i + 1) * 512], b_pv[i][:]).then_inc(s["pT_hi"], 1)

            def u_high(ph, n, half):
                s = att[ph]
                for b in range(2):
                    act.wait_ge(s["pv_ps"], 4 * n + 2 * half + b + 1)
                    copy(U[:, half, 0, :, b * S:(b + 1) * S],
                         b_pv[b][:].rearrange("p (h c) -> p h c", h=NPAIR)).then_inc(s["u_hi"], 1)

            group_of = {}

            def work(ph, g, slot, second, between=()):
                if ph == CROSS:
                    js = range(4, 8) if second else range(4)
                else:
                    js = range(KPAIR + 4, KPAIR + NPAIR) if second else range(KPAIR + 4)
                between = list(between)
                if ph == SELF and not second:
                    read_gram(g)
                for j in js:
                    if between:
                        between.pop(0)()
                    read_pair(ph, g, slot, j)
                    if ph == SELF and j > js[0] + 1:
                        swap_halves(g, slot, j - 1)
                if ph == SELF:
                    swap_halves(g, slot, js[-1])
                if ph == SELF and second:
                    for i in range(GT):
                        read_v(g, slot, i)

            def step(ph, it, t):
                n, gs = it * STEPS + t, it * 2
                probs_high(ph, n)
                ahead = gs + (t // GT + 2 if t % 2 else t // GT + 1)
                slot = (t // GT + (2 if t % 2 else 1)) % 2
                there = is_there(ahead, GROUPS)
                if there and t % 2:
                    rows_high(ph, ahead)
                elif there and ph == CROSS:
                    ctx_copy(ahead, slot)
                if ph == CROSS:
                    stage_mask(n + 2, t % 2)
                t1 = (t + 1) % STEPS
                group_of[t1] = gs + (t + 1) // GT
                more = is_there(n + 1, TILES)
                if ph == CROSS or not there:
                    between = [lambda b=b: exps(ph, n + 1, t1, b) for b in range(2)] if more else []
                    if there:
                        work(ph, ahead, slot, t % 2 == 0, between)
                    else:
                        for f in between:
                            f()
                    u_high(ph, n, 0)
                    u_high(ph, n, 1)
                    return

                def read(*js):
                    for j in js:
                        read_pair(ph, ahead, slot, j)

                def swap(j):
                    swap_halves(ahead, slot, j)

                if t % 2:
                    read_gram(ahead)
                    read(0, 1, 2)
                    exps(ph, n + 1, t1, 0)
                    read(3)
                    exps(ph, n + 1, t1, 1)
                    read(4)
                    swap(1)
                    read(5)
                    u_high(ph, n, 0)
                    swap(2)
                    swap(3)
                    u_high(ph, n, 1)
                    swap(4)
                    swap(5)
                else:
                    read(6, 7)
                    exps(ph, n + 1, t1, 0)
                    read(8)
                    exps(ph, n + 1, t1, 1)
                    read(9)
                    swap(7)
                    read_v(ahead, slot, 0)
                    swap(8)
                    read_v(ahead, slot, 1)
                    u_high(ph, n, 0)
                    swap(9)
                    u_high(ph, n, 1)

            def attention(ph):
                rows_high(ph, 0)
                if ph == CROSS:
                    act.wait_ge(consts_in, N_CONSTS)
                    stage_mask(0, 0)
                    stage_mask(1, 1)
                    ctx_copy(0, 0)
                work(ph, 0, 0, False)
                work(ph, 0, 0, True)
                rows_high(ph, 1)
                work(ph, 1, 1, False)
                group_of[0] = 0
                for b in range(2):
                    exps(ph, 0, 0, b)
                for t in range(STEPS):
                    step(ph, 0, t)
                with act.Fori(1, PASSES - 1) as it:
                    for t in range(STEPS):
                        step(ph, it, t)
                for t in range(STEPS):
                    step(ph, PASSES - 1, t)

            fold_weights()
            attention(CROSS)

            act.wait_ge(pr["normT"], 1)
            splits = [(name, dst[:, 0, k, :], src.rearrange("p (k c) -> p k c", k=KD)[:, k, :], ln_w[:, 0, k:k + 1])
                      for name, dst, src in (("wk", W_k, flat(kT[:, 0])), ("wq", W_q, q_flat[0]),
                                             ("wv", W_v, flat(kT[:, 1]))) for k in range(KD)]
            splits += [("wo", W_o[:, half, 0, :], Wo_raw[:, half, :], 1.0) for half in halves_of_heads]
            assert len(splits) == NPAIR
            for j in range(NPAIR):
                act.wait_ge(pr["gramT_ps"], j + 1)
                need(act, pr["gram_part"], j - 1)
                copy(mask_rot[:, j % 2], b_proj[j % 2][:]).then_inc(pr["gramT"], 1)
                name, dst, src, scale = splits[j]
                act.wait_ge(w_in[name], 16)
                if name == "wo":
                    act.wait_ge(att[CROSS]["out_ps"], TILES)
                copy(dst, src, scale=scale).then_inc(pr["hi_s"], 1)
            act.wait_ge(pr["gram_part"], NPAIR)
            for m in range(KD):
                copy(gram[:, 0, m, :], b_score[m][:, 0:D], scale=ln_w[:, 0, m:m + 1]).then_inc(pr["gram_hi"], 1)
            attention(SELF)

            for name, dst, src in (("wg", W_g, q_flat[0][:, 0:2048]), ("wu", W_u, q_flat[0][:, 2048:4096])):
                act.wait_ge(w_in[name], 32)
                src = src.rearrange("p (k c) -> p k c", k=KD)
                for k in range(KD):
                    copy(dst[:, 0, k, :], src[:, k, :], scale=ln_w[:, 1, k:k + 1]).then_inc(pr["hi_e"], 1)
            act.wait_ge(w_in["wd"], 16)
            act.wait_ge(att[SELF]["out_ps"], TILES)
            copy(W_d[:, 0], q_flat[1][:, 0:2048].rearrange("p (e c) -> p e c", e=E)).then_inc(pr["hi_e"], 1)

            def chunk_scale(c, u):
                act.wait_ge(ex["norm_rows"], CHUNK_NORM_LINKS * (c + 1))
                need(act, ex["T_ps"], c)
                r = rs_y[:].bitcast(F32)
                for i in range(CT):
                    last = copy(yn[:, i, :], yc[:, u, i, :], scale=r[:, i:i + 1])
                last.then_inc(ex["scaled"], 1)

            def chunk_rows(c, u):
                act.wait_ge(ex["T_ps"], c + 1)
                for k, bank in enumerate((b_out, b_misc)):
                    last = copy(h_full[:, u, k, :], bank[:])
                last.then_inc(ex["h_full"], 1)
                for k, bank in enumerate((b_out, b_misc)):
                    last = copy(h2T[:, u, 0, k, :], bank[:])
                last.then_inc(ex["h_hi"], 1)

            def route_exp(c):
                act.wait_ge(ex["rt_ps"], c + 1)
                need(act, ex["routed"], ROUTE_LINKS * c)
                nc.scalar.activation(route[:, 0].rearrange("p t e -> p (t e)"), b_out[:, 0:CT * E], ACT.Exp,
                                     scale=-1.0).then_inc(ex["rt_exp"], 1)

            def chunk_pair(it):
                for u in range(2):
                    c = it * 2 + u
                    for e in range(E):
                        i = c * E + e
                        act.wait_ge(ex["gate_ps"], i + 1)
                        need(act, ex["gated"], i - 1)
                        nc.scalar.activation(th[:, e % 2], b_score[e % 2][:], ACT.Tanh, scale=0.5
                                             ).then_inc(ex["tanh"], 1)
                        if e == 2 and is_there(c + 1, CHUNKS):
                            chunk_scale(c + 1, 1 - u)
                        act.wait_ge(ex["act"], i + 1)
                        need(act, ex["down_ps"], 2 * (i - 1))
                        copy(actT[:, e % 2, 0], act_f[:, e % 2]).then_inc(ex["a_hi"], 1)
                        if e == 3 and is_there(c + 1, CHUNKS):
                            chunk_rows(c + 1, 1 - u)
                        if e == 5 and is_there(c + 1, CHUNKS):
                            route_exp(c + 1)

            chunk_scale(0, 0)
            act.wait_ge(pr["lo_e"], 4)
            chunk_rows(0, 0)
            route_exp(0)
            act.wait_ge(pr["lo_wd"], 1)
            chunk_pair(0)
            with act.Fori(1, CHUNKS // 2 - 1) as it:
                chunk_pair(it)
            chunk_pair(CHUNKS // 2 - 1)

        @block.vector
        def _(dve):
            tt, ts = nc.vector.tensor_tensor, nc.vector.tensor_scalar

            def low(dst, src, high):
                return tt(dst, src, high, ALU.subtract)

            def constants():
                nc.vector.memset(ones_f[:], 1.0)
                nc.vector.memset(k_share[:], float(H // KVS))
                for i in (0, K_BLOCKS - 1):
                    nc.vector.memset(k_blocks[:, i, :], 0.0)
                nc.vector.memset(ones_row[:], 1.0)
                dve.wait_ge(eye_in, 16)
                for i in range(2):
                    nc.vector.tensor_copy(eye2_b[:, i, :], eye_f[0:S, 0:S])
                dve.wait_ge(consts_in, N_CONSTS)
                nc.vector.tensor_copy(causal_b[:], causal_f[:])
                nc.vector.reduce_max(any_valid[:], mask_all.rearrange("p (b s) -> p b s", b=B), AX_X
                                     ).then_inc(pr["consts"], 1)

            def fold_weights():
                for j in range(NPAIR):
                    dve.wait_ge(pr["fold_hi"], 2 * j + 1)
                    cols = slice(2 * j * HD, 2 * (j + 1) * HD)
                    for i in range(2):
                        hc = slice((2 * j + i) * HD, (2 * j + i + 1) * HD)
                        last = low(W_q[:, 1, :, hc],
                                   (b_out, b_misc)[j % 2][:, i * D:(i + 1) * D].rearrange("p (k c) -> p k c", k=KD),
                                   W_q[:, 0, :, hc])
                    last.then_inc(pr["fold_lo"], 1)
                    dve.wait_ge(pr["fold_hi"], 2 * j + 2)
                    low(W_o[:, 2 * j:2 * j + 2, 1, :], b_score[j % 2][:].rearrange("p (h c) -> p h c", h=2),
                        W_o[:, 2 * j:2 * j + 2, 0, :]).then_inc(pr["fold_lo"], 1)

            def statistics(ch, rows):
                n = len(rows)
                for i in range(n):
                    last = nc.vector.bn_stats(stat6[:, i, :], rows[i])
                ch.link(last)
                dve.nop(nofuse=True)
                for i in range(n):
                    last = nc.vector.bn_aggr(stat[:, i, :], stat6[:, i, :])
                ch.link(last)

            def mean_squares(ch, n, dst):
                mean, var = stat[:, 0:n, 0], stat[:, 0:n, 1]
                ch.link(tt(rs_t[:, 0:n], mean, mean, ALU.mult))
                ch.link(nc.vector.scalar_tensor_tensor(out=dst, in0=rs_t[:, 0:n], scalar=RMS_EPS, in1=var,
                                                       op0=ALU.add, op1=ALU.add))

            def norm_group(g, slot, uses):
                s = att[CROSS]
                dve.wait_ge(s[f"x_in{slot}"], 16 * uses)
                ch = Chain(dve, s["norm_rows"], g, NORM_LINKS[CROSS])
                statistics(ch, [xin[:, slot, i, :] for i in range(GT)])
                r = rsqrt(ch, stat[:, 0:GT, 1], rs_v, rs_t, rs_y, GT, LN_EPS)
                need(dve, s["hT_ps"], g)
                for i in range(GT):
                    last = ts(xn[:, i, :], xin[:, slot, i, :], stat[:, i, 0:1], r[:, i:i + 1], ALU.subtract, ALU.mult)
                ch.last(last)

            def scales(g, slot, uses, there=True):
                s = att[SELF]
                ch = Chain(dve, s["scales"], g, SCALE_LINKS)
                n = 3 * GT
                before_ = type(g) is not int or g > 0
                if before_:
                    dve.wait_ge(s["squares_ps"], g)
                    ins = ts(rs_v[:, 0:n], b_misc[:, 0:n], 1.0 / (H * HD), RMS_EPS, ALU.mult, ALU.add)
                    if not there:
                        ch.link(ins)
                if there:
                    dve.wait_ge(s[f"x_in{slot}"], 16 * uses)
                    statistics(ch, [xin[:, slot, i, :] for i in range(GT)])
                    mean_squares(ch, GT, rs_v[:, n:n + GT])
                cols = slice(0 if before_ else n, n + GT if there else n)
                rsqrt(ch, None, *(a[:, cols] for a in (rs_v, rs_t, rs_y)), cols.stop - cols.start)
                r = rs_y[:].bitcast(F32)
                if before_:
                    for i in range(GT):
                        ts(diag[:, i, :], eye_f[:], r[:, i:i + 1], None, ALU.mult)
                    ts(q_factor[:, 1 - slot, :], r[:, GT:n], SCORE_SCALE, None, ALU.mult).then_inc(s["factors"], 1)
                if there:
                    for i in range(GT):
                        last = ts(xn[:, i, :], xin[:, slot, i, :], r[:, n + i:n + i + 1], None, ALU.mult)
                    last.then_inc(s["norm_rows"], 1)

            def rows_low(ph, g):
                s = att[ph]
                dve.wait_ge(s["hT_hi"], g + 1)
                low(hT[:, 1], b_misc[:].rearrange("p (k c) -> p k c", k=KD), hT[:, 0]).then_inc(s["hT_lo"], 1)

            def softmax_shift(ph, n, t):
                s = att[ph]
                for b in range(2):
                    dve.wait_ge(s["score_ps"], 2 * n + b + 1)
                    m, src = mx[:, t % 2, b, :], pairs_of(b_score[b][:])
                    nc.vector.reduce_max(m, src, AX_X).then_inc(s["row_max"], 1)
                    dve.wait_ge(s["row_max"], 2 * n + b + 1)
                    tt(prob[:, t % 2, :, b, :], src, m.unsqueeze(2).to_broadcast([P, NPAIR, S]),
                       ALU.subtract).then_inc(s["shifted"], 1)

            def softmax_sum(ph, n, t):
                s = att[ph]
                ch = Chain(dve, s["row_sum"], n, SUM_LINKS[ph])
                for b in range(2):
                    dve.wait_ge(s["expd"], 2 * n + b + 1)
                    last = nc.vector.reduce_sum(sm[:, t % 2, b, :], prob[:, t % 2, :, b, :], AX_X)
                ch.link(last)
                r = sm[:, t % 2]
                if ph == CROSS:
                    ch.link(nc.vector.reciprocal(r, r))
                    ch.last(tt(r, r, any_valid[:, bass.ds(n * 2, 2)].unsqueeze(2).to_broadcast([P, 2, NPAIR]),
                               ALU.mult))
                else:
                    ch.last(nc.vector.reciprocal(r, r))

            def probs_low(ph, n):
                s = att[ph]
                for i in range(2):
                    dve.wait_ge(s["pT_hi"], 2 * n + i + 1)
                    low(PT[:, 1, i * 512:(i + 1) * 512], b_pv[i][:], PT[:, 0, i * 512:(i + 1) * 512]
                        ).then_inc(s["pT_lo"], 1)

            def u_low(ph, n, half):
                s = att[ph]
                for b in range(2):
                    dve.wait_ge(s["u_hi"], 4 * n + 2 * half + b + 1)
                    c = slice(b * S, (b + 1) * S)
                    low(U[:, half, 1, :, c], b_pv[b][:].rearrange("p (h c) -> p h c", h=NPAIR),
                        U[:, half, 0, :, c]).then_inc(s["u_lo"], 1)

            def tail_sum(ph, n, t, it):
                s = att[ph]
                slot = t // GT % 2
                ch = Chain(dve, s["tail"], n, TAIL_LINKS[ph])
                dve.wait_ge(s["out_ps"], n + 1)
                dve.wait_ge(s[f"r_in{slot}"], 16 * (it + 1))
                need(dve, s[f"sum_st{t % 2}"], 16 * (it * 2 + t // 2))
                ch.link(tt(half_sum[:], b_out[:, 0:D], res[:, slot, t % GT, :], ALU.add))
                total_ = tt(summed[:, t % 2, :], b_out[:, D:2 * D], half_sum[:], ALU.add)
                if ph == SELF:
                    ch.last(total_)
                else:
                    ch.link(total_)
                return ch

            def tail_norm(ch, t, it):
                s = att[CROSS]
                ch.link(nc.vector.bn_stats(tstat6[:], summed[:, t % 2, :]))
                dve.nop(nofuse=True)
                ch.link(nc.vector.bn_aggr(tstat[:], tstat6[:]))
                r = rsqrt(ch, tstat[:, 1:2], ts_v, ts_t, ts_y, 1, LN_EPS)
                need(dve, s[f"ln_st{t % 2}"], 16 * (it * 2 + t // 2))
                ch.last(ts(ln_out[:, t % 2, :], summed[:, t % 2, :], tstat[:, 0:1], r, ALU.subtract, ALU.mult))

            def h_times_gram(g):
                s = att[SELF]
                dve.wait_ge(s["gram_ev"], g + 1)
                tt(flat(xn[:]), flat(xn[:]), b_misc[:], ALU.mult).then_inc(s["h_gram"], 1)

            def turn(g, slot, js):
                s = att[SELF]
                for j in js:
                    i = turn_of(j)
                    dve.wait_ge(s["swap"], TURNS * g + i + 1)
                    h = 2 * j if j < KPAIR else 2 * (j - KPAIR)
                    v = (k_pair if j < KPAIR else q_pair)(slot, h)[0:RD]
                    tt(v, v, by_batch(cos_t[:]), ALU.mult)
                    need(dve, s["rotated"], ROTS * g + j - 1)
                    tt(rot[:, j % 2].rearrange("p (b h c) -> p b h c", h=2, c=S),
                       swapped[:, i % 2].rearrange("p (b h c) -> p b h c", h=2, c=S), by_batch(sin_t), ALU.mult
                       ).then_inc(s["turned"], 1)

            def k_scale(g, slot):
                s = att[SELF]
                dve.wait_ge(s["rkb_ps"], g + 1)
                dve.wait_ge(s["rotated"], ROTS * g + KPAIR)
                tt(kT[:, slot], kT[:, slot], b_misc[:, GTOK:2 * GTOK].unsqueeze(1).to_broadcast([P, KVS, GTOK]),
                   ALU.mult).then_inc(s["k_scaled"], 1)

            def v_low(g, gslot):
                s = att[SELF]
                for i in range(GT):
                    j = KPAIR + NPAIR + i
                    dve.wait_ge(s["proj_ev"], PROJ[SELF] * g + j + 1)
                    low(V[:, GT * gslot + i, 1, :], proj_bank(SELF, j)[:], V[:, GT * gslot + i, 0, :]
                        ).then_inc(s["v_lo"], 1)

            def step(ph, it, t):
                n, gs = it * STEPS + t, it * 2
                ahead = gs + (t // GT + 2 if t % 2 else t // GT + 1)
                slot = (t // GT + (2 if t % 2 else 1)) % 2
                there, more = is_there(ahead, GROUPS), is_there(n + 1, TILES)
                probs_low(ph, n)
                if ph == SELF and there and t % 2 == 0:
                    scales(ahead + 1, 1 - slot, it + 2, is_there(ahead + 1, GROUPS))
                if there and t % 2:
                    rows_low(ph, ahead)
                if more:
                    softmax_shift(ph, n + 1, (t + 1) % STEPS)
                if ph == SELF and there and t % 2:
                    h_times_gram(ahead)
                if more:
                    softmax_sum(ph, n + 1, (t + 1) % STEPS)
                if ph == SELF and there:
                    turn(ahead, slot, range(1, 2) if t % 2 else range(7, 8))
                if ph == CROSS and t % 2 == 0 and is_there(ahead + 1, GROUPS):
                    norm_group(ahead + 1, 1 - slot, it + 2)
                u_low(ph, n, 0)
                if ph == SELF and there and t % 2 == 0:
                    turn(ahead, slot, range(8, 9))
                before_ = (t - 1) % STEPS, it - (1 if t == 0 else 0)
                ch = None
                if type(n) is not int or n > 0:
                    ch = tail_sum(ph, n - 1, *before_)
                if ph == SELF and there:
                    turn(ahead, slot, range(2, 3) if t % 2 else range(9, 10))
                u_low(ph, n, 1)
                if ph == SELF and there:
                    if t % 2:
                        turn(ahead, slot, range(3, 6))
                    else:
                        k_scale(ahead, slot)
                        v_low(ahead, slot)
                if ch and ph == CROSS:
                    tail_norm(ch, *before_)

            def attention(ph):
                if ph == CROSS:
                    norm_group(0, 0, 1)
                    rows_low(ph, 0)
                    norm_group(1, 1, 1)
                    rows_low(ph, 1)
                else:
                    rows_low(ph, 0)
                    h_times_gram(0)
                    turn(0, 0, range(1, 6))
                    scales(1, 1, 1)
                    turn(0, 0, range(7, 10))
                    k_scale(0, 0)
                    v_low(0, 0)
                    rows_low(ph, 1)
                    h_times_gram(1)
                    turn(1, 1, range(1, 6))
                softmax_shift(ph, 0, 0)
                softmax_sum(ph, 0, 0)
                for t in range(STEPS):
                    step(ph, 0, t)
                with dve.Fori(1, PASSES - 1) as it:
                    for t in range(STEPS):
                        step(ph, it, t)
                for t in range(STEPS):
                    step(ph, PASSES - 1, t)
                ch = tail_sum(ph, TILES - 1, STEPS - 1, PASSES - 1)
                if ph == CROSS:
                    tail_norm(ch, STEPS - 1, PASSES - 1)

            constants()
            fold_weights()
            dve.wait_ge(pr["consts"], 1)
            attention(CROSS)

            for a, (dst, src) in enumerate(((W_k, flat(kT[:, 0])), (W_q, q_flat[0]), (W_v, flat(kT[:, 1])))):
                src = src.rearrange("p (k c) -> p k c", k=KD)
                for k in range(KD):
                    dve.wait_ge(pr["hi_s"], 2 * a + k + 1)
                    nc.vector.scalar_tensor_tensor(out=dst[:, 1, k, :], in0=src[:, k, :], scalar=ln_w[:, 0, k:k + 1],
                                                   in1=dst[:, 0, k, :], op0=ALU.mult, op1=ALU.subtract
                                                   ).then_inc(pr["lo_s"], 1)
            scales(0, 0, 1)
            for m in range(KD):
                dve.wait_ge(pr["gram_hi"], m + 1)
                nc.vector.scalar_tensor_tensor(out=gram[:, 1, m, :], in0=b_score[m][:, 0:D],
                                               scalar=ln_w[:, 0, m:m + 1], in1=gram[:, 0, m, :],
                                               op0=ALU.mult, op1=ALU.subtract).then_inc(pr["gram_lo"], 1)
            attention(SELF)

            for k in range(KD):
                last = ts(rt_w[:, k, :], rt_raw[:, k, :], ln_w[:, 1, k:k + 1], None, ALU.mult)
            last.then_inc(pr["rt_w"], 1)
            for a, (dst, src) in enumerate(((W_g, q_flat[0][:, 0:2048]), (W_u, q_flat[0][:, 2048:4096]))):
                src = src.rearrange("p (k c) -> p k c", k=KD)
                for k in range(KD):
                    dve.wait_ge(pr["hi_e"], 2 * a + k + 1)
                    nc.vector.scalar_tensor_tensor(out=dst[:, 1, k, :], in0=src[:, k, :], scalar=ln_w[:, 1, k:k + 1],
                                                   in1=dst[:, 0, k, :], op0=ALU.mult, op1=ALU.subtract
                                                   ).then_inc(pr["lo_e"], 1)

            def chunk_statistics(c, u, uses):
                ch = Chain(dve, ex["norm_rows"], c, CHUNK_NORM_LINKS)
                dve.wait_ge(ex[f"y_in{u}"], 16 * uses)
                need(dve, ex["scaled"], c)
                statistics(ch, [yc[:, u, i, :] for i in range(CT)])
                mean_squares(ch, CT, rs_v[:, 0:CT])
                return ch

            def chunk_rms(ch):
                rsqrt(ch, None, rs_v, rs_t, rs_y, CT)

            def chunk_low(c, u):
                dve.wait_ge(ex["h_hi"], c + 1)
                for k, bank in enumerate((b_out, b_misc)):
                    last = low(h2T[:, u, 1, k, :], bank[:], h2T[:, u, 0, k, :])
                last.then_inc(ex["h_lo"], 1)

            sig, val, cnt, picked = (route[:, i] for i in range(4))

            def rank_experts(c):
                ch = Chain(dve, ex["routed"], c, ROUTE_LINKS)
                dve.wait_ge(ex["rt_exp"], c + 1)
                gt, eq = (rank3[:, i].rearrange("p t (e f) -> p t e f", e=E) for i in range(2))
                ch.link(ts(sig, sig, 1.0, None, ALU.add))
                ch.link(nc.vector.reciprocal(sig, sig))
                ch.link(tt(val, sig, rt_bias[:].unsqueeze(1).to_broadcast([P, CT, E]), ALU.add))
                other = val.unsqueeze(2).to_broadcast([P, CT, E, E])
                own = val.unsqueeze(3).to_broadcast([P, CT, E, E])
                ch.link(tt(gt, other, own, ALU.is_gt))
                ch.link(tt(eq, other, own, ALU.is_equal))
                ch.link(tt(eq, eq, before[:].unsqueeze(1).to_broadcast([P, CT, E, E]), ALU.mult))
                ch.link(tt(gt, gt, eq, ALU.add))
                ch.link(nc.vector.reduce_sum(cnt, gt, AX_X))
                return ch

            def top_experts(ch, u):
                sums, inv = route[:, 4, :, 0], route[:, 4, :, 1]
                ch.link(nc.vector.scalar_tensor_tensor(out=picked, in0=cnt, scalar=float(TOPK), in1=sig,
                                                       op0=ALU.is_lt, op1=ALU.mult))
                ch.link(nc.vector.reduce_sum(sums, picked, AX_X))
                ch.link(nc.vector.reciprocal(inv, sums))
                ch.last(nc.vector.scalar_tensor_tensor(out=comb[:, u], in0=picked, scalar=0.5,
                                                       in1=inv.unsqueeze(2).to_broadcast([P, CT, E]),
                                                       op0=ALU.mult, op1=ALU.mult))

            def add_expert(i, u, e):
                for b in range(2):
                    dve.wait_ge(ex["down_ps"], 2 * i + b + 1)
                    for a in range(2):
                        tile = 2 * b + a
                        if e > 0:
                            dve.wait_ge(ex["added"], CT * (i - 1) + tile + 1)
                        nc.vector.scalar_tensor_tensor(
                            out=total[:, u, tile, :], in0=b_proj[b][:, a * D:(a + 1) * D],
                            scalar=comb[:, u, tile, e:e + 1], in1=total[:, u, tile, :],
                            op0=ALU.mult, op1=ALU.add).then_inc(ex["added"], 1)

            def chunk_pair(it):
                for u in range(2):
                    c = it * 2 + u
                    for e in range(E):
                        i = c * E + e
                        dve.wait_ge(ex["tanh"], i + 1)
                        nc.vector.scalar_tensor_tensor(out=gated[:, e % 2], in0=th[:, e % 2], scalar=1.0,
                                                       in1=b_score[e % 2][:], op0=ALU.add, op1=ALU.mult
                                                       ).then_inc(ex["gated"], 1)
                        dve.wait_ge(ex["gated"], i + 1)
                        dve.wait_ge(ex["up_ps"], i + 1)
                        need(dve, ex["a_lo"], i - 1)
                        tt(act_f[:, e % 2], gated[:, e % 2], b_pv[e % 2][:], ALU.mult).then_inc(ex["act"], 1)
                        if type(i) is not int or i > 0:
                            if e == 1:
                                dve.wait_ge(ex["init"], c + 1)
                                dve.wait_ge(ex["routed"], ROUTE_LINKS * (c + 1))
                            add_expert(i - 1, u if e else 1 - u, (e - 1) % E)
                        if not is_there(c + 1, CHUNKS):
                            continue
                        if e == 0:
                            ch = chunk_statistics(c + 1, 1 - u, it + 1 + (1 if u else 0))
                        elif e == 1:
                            chunk_rms(ch)
                        elif e == 4:
                            chunk_low(c + 1, 1 - u)
                        elif e == 6:
                            ch = rank_experts(c + 1)
                        elif e == 7:
                            top_experts(ch, 1 - u)

            chunk_rms(chunk_statistics(0, 0, 1))
            chunk_low(0, 0)
            top_experts(rank_experts(0), 0)
            dve.wait_ge(pr["lo_wd"], 1)
            chunk_pair(0)
            with dve.Fori(1, CHUNKS // 2 - 1) as it:
                chunk_pair(it)
            chunk_pair(CHUNKS // 2 - 1)
            add_expert(CHUNKS * E - 1, 1, E - 1)

        @block.gpsimd
        def _(pool):
            tt = nc.gpsimd.tensor_tensor

            def split_ctx(g, slot):
                s = att[CROSS]
                dst = V[:, GT * slot:GT * (slot + 1)]
                pool.wait_ge(s["c_hi"], g + 1)
                tt(dst[:, :, 1, 0:DV], ctx_raw[:, slot], dst[:, :, 0, 0:DV], ALU.subtract).then_inc(s["c_lo"], 1)

            def normalise(ph, n, t):
                s = att[ph]
                pool.wait_ge(s["row_sum"], SUM_LINKS[ph] * (n + 1))
                for b in range(2):
                    p = prob[:, t % 2, :, b, :]
                    tt(p, p, sm[:, t % 2, b, :].unsqueeze(2).to_broadcast([P, NPAIR, S]), ALU.mult
                       ).then_inc(s["probs"], 1)

            def rotate(g, slot, js):
                s = att[SELF]
                for j in js:
                    r = ROTS * g + j
                    h = 2 * j if j < KPAIR else 2 * (j - KPAIR)
                    v = (k_pair if j < KPAIR else q_pair)(slot, h)[0:RD]
                    sines = rot[:, j % 2].rearrange("p (b h c) -> p b h c", h=2, c=S)
                    if j in POOL_PAIRS:
                        pool.wait_ge(s["proj_ev"], PROJ[SELF] * g + j + 1)
                        need(pool, s["rotated"], r)
                        done = 3 * (len(POOL_PAIRS) * g + POOL_PAIRS.index(j))
                        for i, (a, b) in enumerate(((0, HALF), (HALF, 0))):
                            tt(sines[a:a + HALF], v[b:b + HALF], by_batch(sin_read[b:b + HALF]), ALU.mult
                               ).then_inc(s["crossed"], 1)
                            pool.wait_ge(s["crossed"], done + i + 1)
                        tt(v, v, by_batch(cos_t[:]), ALU.mult).then_inc(s["crossed"], 1)
                        pool.wait_ge(s["crossed"], done + 3)
                    else:
                        pool.wait_ge(s["turned"], TURNS * g + turn_of(j) + 1)
                    tt(v, v, sines, ALU.add).then_inc(s["rotated"], 1)

            def add_squares(g):
                s = att[SELF]
                pool.wait_ge(s["proj_ev"], PROJ[SELF] * g + KPAIR)
                tt(k_sq[:, 0], k_sq[:, 0], k_sq[:, 1], ALU.add).then_inc(s["sq_added"], 1)
                pool.wait_ge(s["h_gram"], g + 1)
                pool.wait_ge(s["sq_added"], 2 * g + 1)
                part = [flat(xn[:])[:, k * GTOK:(k + 1) * GTOK].rearrange("p (b c) -> p b c", c=S).unsqueeze(2)
                        .to_broadcast([P, 2 * GT, 2, S]) for k in range(KD)]
                tt(k_sq[:, 1].rearrange("p (b r c) -> p b r c", r=2, c=S), part[0], part[1], ALU.add
                   ).then_inc(s["sq_added"], 1)

            def step(ph, it, t):
                n, gs = it * STEPS + t, it * 2
                ahead = gs + (t // GT + 2 if t % 2 else t // GT + 1)
                slot = (t // GT + (2 if t % 2 else 1)) % 2
                there = is_there(ahead, GROUPS)
                if there and ph == CROSS and t % 2 == 0:
                    split_ctx(ahead, slot)
                if there and ph == SELF:
                    rotate(ahead, slot, range(0, 1) if t % 2 else range(6, 7))
                if is_there(n + 1, TILES):
                    normalise(ph, n + 1, (t + 1) % STEPS)
                if there and ph == SELF:
                    if t % 2:
                        rotate(ahead, slot, range(1, 2))
                        add_squares(ahead)
                        rotate(ahead, slot, range(2, 6))
                    else:
                        rotate(ahead, slot, range(7, 10))

            def attention(ph):
                if ph == CROSS:
                    split_ctx(0, 0)
                else:
                    for g in range(2):
                        rotate(g, g, range(0, 2))
                        add_squares(g)
                        rotate(g, g, range(2, 6 if g else 10))
                normalise(ph, 0, 0)
                for t in range(STEPS):
                    step(ph, 0, t)
                with pool.Fori(1, PASSES - 1) as it:
                    for t in range(STEPS):
                        step(ph, it, t)
                for t in range(STEPS):
                    step(ph, PASSES - 1, t)

            attention(CROSS)
            for i, half in enumerate(halves_of_heads):
                pool.wait_ge(pr["hi_s"], 7 + i)
                tt(W_o[:, half, 1, :], Wo_raw[:, half, :], W_o[:, half, 0, :], ALU.subtract).then_inc(pr["lo_wo"], 1)
            pool.wait_ge(pr["lo_wo"], 2)
            attention(SELF)
            pool.wait_ge(pr["hi_e"], 5)
            tt(W_d[:, 1], q_flat[1][:, 0:2048].rearrange("p (e c) -> p e c", e=E), W_d[:, 0], ALU.subtract
               ).then_inc(pr["lo_wd"], 1)
            pool.wait_ge(pr["lo_e"], 4)
            pool.wait_ge(pr["lo_wd"], 1)

            def begin_total(c, u, uses):
                pool.wait_ge(ex[f"x_in{u}"], 16 * uses)
                pool.wait_ge(ex[f"y_in{u}"], 16 * uses)
                need(pool, ex[f"st{u}"], 16 * (uses - 1))
                tt(total[:, u], xc[:, u], yc[:, u], ALU.add).then_inc(ex["init"], 1)

            def chunk_pair(it):
                for u in range(2):
                    c = it * 2 + u
                    for e in range(E):
                        i = c * E + e
                        pool.wait_ge(ex["a_hi"], i + 1)
                        tt(actT[:, e % 2, 1], act_f[:, e % 2], actT[:, e % 2, 0], ALU.subtract
                           ).then_inc(ex["a_lo"], 1)
                        if e == 4 and is_there(c + 1, CHUNKS):
                            begin_total(c + 1, 1 - u, it + 1 + (1 if u else 0))

            begin_total(0, 0, 1)
            chunk_pair(0)
            with pool.Fori(1, CHUNKS // 2 - 1) as it:
                chunk_pair(it)
            chunk_pair(CHUNKS // 2 - 1)


_INS = ['x', 'ctx_1024', 'mask_BxS2_bf1', 'L0_xattn_Wq', 'L0_xattn_Wk', 'L0_xattn_Wv', 'L0_xattn_Wo',
        'L0_ffn_ln1_w', 'L0_ffn_ln2_w', 'L0_ffn_wq', 'L0_ffn_wk', 'L0_ffn_wv', 'L0_ffn_wo',
        'L0_ffn_qnorm_w', 'L0_ffn_knorm_w', 'L0_ffn_router_w', 'L0_ffn_router_bias', 'L0_ffn_wg',
        'L0_ffn_wu', 'L0_ffn_wd']
_ROWS = ('x', 'ctx_1024')


def shape_constants():
    import numpy as np

    f = np.float32
    inv_freq = (f(1.0) / f(1000000.0) ** (np.arange(0, RD, 2, dtype=f) / f(RD))).astype(f)
    ang = np.arange(S, dtype=f)[None, :] * inv_freq[:, None]
    cos = np.tile(np.cos(ang).astype(f), (2, GTOK // S))
    sin = np.tile(np.sin(ang).astype(f), (1, GTOK // S))
    rope = np.stack([cos, np.concatenate([sin, -sin]), np.concatenate([-sin, sin])])
    causal = np.where(np.tril(np.ones((S, S), bool)), f(0.0), f(MASKED)).astype(f)
    earlier = np.tril(np.ones((E, E), f), -1).reshape(1, E * E)
    return {"eye": np.eye(P, dtype=f), "rope": rope.astype(f), "causal": causal, "earlier": earlier}


def kernel(**inputs):
    import numpy as _np
    import concourse.bacc as _bacc
    from concourse import mybir as _mybir
    from concourse.bass_utils import run_bass_kernel_spmd as _run

    nc = _bacc.Bacc("TRN2", target_bir_lowering=False, num_devices=1)
    arrays, args = {}, []

    def give(name, a):
        arrays[f"in_{name}_dram"] = a
        args.append(nc.dram_tensor(f"in_{name}_dram", a.shape, _mybir.dt.from_np(a.dtype), kind="ExternalInput").ap())

    for name in _INS:
        a = _np.ascontiguousarray(inputs[name])
        if a.dtype == bool:
            a = a.view(_np.uint8)
        if name in _ROWS:
            a = a.reshape(-1, a.shape[-1])
        give(name, a)
    for name, a in shape_constants().items():
        give(name, a)
    out = nc.dram_tensor("out_dram", (B * S, D), F32, kind="ExternalOutput").ap()
    build(nc, *args, out)
    r = _run(nc, [arrays], core_ids=[0])
    return r.results[0]["out_dram"].reshape(B, S, D)
```
